# Optimizing a Trainium2 kernel written in Bass

```python
import numpy as np
import jax
import jax.numpy as jnp

def _softmax(x, axis=-1):
    return jax.nn.softmax(x, axis=axis)

def _gelu(x):
    return jax.nn.gelu(x, approximate=True)

def _silu(x):
    return jax.nn.silu(x)

def _sigmoid(x):
    return jax.nn.sigmoid(x)

def _layernorm(x, axis=-1, eps=1e-05):
    m = jnp.mean(x, axis=axis, keepdims=True)
    v = jnp.var(x, axis=axis, keepdims=True)
    return (x - m) / jnp.sqrt(v + eps)

def _scatter_add(tgt, idx, src, axis=0):
    return tgt.at[idx].add(src)

def _segment_sum(src, seg, n):
    return jax.ops.segment_sum(src, seg, n)
kernel_name = 'mk_adj_seq_d4_adj_r2_d52a58'

def setup_inputs(seed: int=0):
    np.random.seed(seed)
    _w = jnp.asarray

    def _rec_inputs():
        import jax
        import jax.numpy as jnp
        _gk = jax.random.key(seed)
        x = -0.0005207 + 1.001 * jax.random.normal(jax.random.fold_in(_gk, 1), (64, 128, 256), jnp.float32)
        _w = (1.0 + jnp.arange(128, dtype=jnp.float32)) ** (-0.5)
        _w = _w / _w.mean()
        _pij = jnp.clip(0.0625 * _w[:, None] * _w[None, :], 0.0, 1.0)
        _a = jax.random.uniform(jax.random.fold_in(_gk, 2), (64, 128, 128)) < _pij
        _a = jnp.logical_or(_a, jnp.eye(128, dtype=bool))
        adj = _a.astype(jnp.int32)
        return (x, adj)
    x, adj = _rec_inputs()

    def _L0_gnn_setup():
        import jax, jax.numpy as jnp
        import numpy as np
        B, S, D, H = (2, 1024, 256, 8)
        HD = D // H
        EPS = 1e-05

        def _ln(x, g, b):
            mu = jnp.mean(x, axis=-1, keepdims=True)
            var = jnp.mean((x - mu) ** 2, axis=-1, keepdims=True)
            return (x - mu) * jax.lax.rsqrt(var + EPS) * g + b
        key = jax.random.key(seed)
        ks = jax.random.split(key, 16)
        x = jax.random.normal(ks[0], (B, S, D), dtype=jnp.float32)
        adj = jax.random.randint(ks[1], (B, S, S), 0, 2, dtype=jnp.int32)
        adj = adj.at[:, jnp.arange(S), jnp.arange(S)].set(1)
        edge_attr = jax.random.normal(ks[2], (B, S, S), dtype=jnp.float32)
        sc = 1.0 / np.sqrt(D)
        p = lambda k, shp: jax.random.normal(k, shp, dtype=jnp.float32) * sc
        return {'x': x, 'adj_matrix': adj, 'edge_attr_matrix': edge_attr, 'ln1_g': jnp.ones((D,)), 'ln1_b': jnp.zeros((D,)), 'ln2_g': jnp.ones((D,)), 'ln2_b': jnp.zeros((D,)), 'wq': p(ks[3], (D, D)), 'bq': jnp.zeros((D,)), 'wk': p(ks[4], (D, D)), 'bk': jnp.zeros((D,)), 'wv': p(ks[5], (D, D)), 'bv': jnp.zeros((D,)), 'wo': p(ks[6], (D, D)), 'bo': jnp.zeros((D,)), 'w1': p(ks[7], (D, 4 * D)), 'b1': jnp.zeros((4 * D,)), 'w2': p(ks[8], (4 * D, D)), 'b2': jnp.zeros((D,))}
    _L0_gnn_all = _L0_gnn_setup()
    _L0_gnn_in = {k: v for k, v in _L0_gnn_all.items() if k in ('ln1_g', 'ln1_b', 'ln2_g', 'ln2_b', 'wq', 'bq', 'wk', 'bk', 'wv', 'bv', 'wo', 'bo', 'w1', 'b1', 'w2', 'b2')}
    del _L0_gnn_all

    def _L1_gnn_setup():
        import jax, jax.numpy as jnp
        import numpy as np
        B, N, E, FF, L = (8, 1024, 256, 128, 2)
        LN_EPS = 1e-05
        SCALE = float(np.sqrt(FF))

        def layer_norm(x, g, b):
            m = jnp.mean(x, axis=-1, keepdims=True)
            v = jnp.mean(jnp.square(x - m), axis=-1, keepdims=True)
            return (x - m) * jax.lax.rsqrt(v + LN_EPS) * g + b
        key = jax.random.key(seed)
        ks = jax.random.split(key, 9)
        s = 0.02
        node_fts = jax.random.normal(ks[0], (B, N, E), jnp.float32)
        rel_edges = jax.random.randint(ks[1], (B, N, N), 0, 2, jnp.int32)
        Wq = jax.random.normal(ks[2], (L, FF, E), jnp.float32) * s
        bq = jnp.zeros((L, FF), jnp.float32)
        Wk = jax.random.normal(ks[3], (L, FF, E), jnp.float32) * s
        bk = jnp.zeros((L, FF), jnp.float32)
        Wc = jax.random.normal(ks[4], (L, E, E), jnp.float32) * s
        ln_g = jnp.ones((L, E), jnp.float32)
        ln_b = jnp.zeros((L, E), jnp.float32)
        return {'node_fts': node_fts, 'rel_edges': rel_edges, 'Wq': Wq, 'bq': bq, 'Wk': Wk, 'bk': bk, 'Wc': Wc, 'ln_g': ln_g, 'ln_b': ln_b}
    _L1_gnn_all = _L1_gnn_setup()
    _L1_gnn_in = {k: v for k, v in _L1_gnn_all.items() if k in ('Wq', 'bq', 'Wk', 'bk', 'Wc', 'ln_g', 'ln_b')}
    del _L1_gnn_all

    def _L2_gnn_setup():
        import jax, jax.numpy as jnp
        import numpy as np
        B, N, D, H = (4, 1024, 256, 8)
        HD = D // H
        EPS = 1e-05
        key = jax.random.key(seed)
        ks = jax.random.split(key, 12)
        x = jax.random.normal(ks[0], (B, N, D), dtype=jnp.float32)
        adj = jax.random.randint(ks[1], (B, N, N), 0, 2, dtype=jnp.int32)
        adj = jnp.maximum(adj, jnp.eye(N, dtype=jnp.int32)[None, :, :])
        s = 1.0 / np.sqrt(D)
        Wq = jax.random.uniform(ks[2], (D, D), jnp.float32, -s, s)
        bq = jnp.zeros((D,), jnp.float32)
        Wk = jax.random.uniform(ks[3], (D, D), jnp.float32, -s, s)
        bk = jnp.zeros((D,), jnp.float32)
        Wv = jax.random.uniform(ks[4], (D, D), jnp.float32, -s, s)
        bv = jnp.zeros((D,), jnp.float32)
        Wo = jax.random.uniform(ks[5], (D, D), jnp.float32, -s, s)
        bo = jnp.zeros((D,), jnp.float32)
        gamma = jnp.ones((D,), jnp.float32)
        beta = jnp.zeros((D,), jnp.float32)
        return {'x': x, 'adj': adj, 'Wq': Wq, 'bq': bq, 'Wk': Wk, 'bk': bk, 'Wv': Wv, 'bv': bv, 'Wo': Wo, 'bo': bo, 'gamma': gamma, 'beta': beta}
    _L2_gnn_all = _L2_gnn_setup()
    _L2_gnn_in = {k: v for k, v in _L2_gnn_all.items() if k in ('Wq', 'bq', 'Wk', 'bk', 'Wv', 'bv', 'Wo', 'bo', 'gamma', 'beta')}
    del _L2_gnn_all

    def _L3_gnn_setup():
        import jax, jax.numpy as jnp
        import numpy as np
        import math
        D = 256
        B, L = (8, 1024)
        EPS = 1e-05

        def layer_norm(y, gamma, beta):
            mu = jnp.mean(y, axis=-1, keepdims=True)
            var = jnp.mean(jnp.square(y - mu), axis=-1, keepdims=True)
            return (y - mu) * jax.lax.rsqrt(var + EPS) * gamma + beta
        key = jax.random.key(seed)
        ks = jax.random.split(key, 8)
        s = 1.0 / math.sqrt(D)
        x = jax.random.normal(ks[0], (B, L, D), dtype=jnp.float32)
        adj = jax.random.randint(ks[1], (B, L, L), 0, 2, dtype=jnp.int32)
        Wq = jax.random.normal(ks[2], (D, D), dtype=jnp.float32) * s
        Wk = jax.random.normal(ks[3], (D, D), dtype=jnp.float32) * s
        Wv = jax.random.normal(ks[4], (D, D), dtype=jnp.float32) * s
        Wo = jax.random.normal(ks[5], (D, D), dtype=jnp.float32) * s
        bo = jnp.zeros((D,), dtype=jnp.float32)
        gamma = jnp.ones((D,), dtype=jnp.float32)
        beta = jnp.zeros((D,), dtype=jnp.float32)
        return {'x': x, 'adj': adj, 'Wq': Wq, 'Wk': Wk, 'Wv': Wv, 'Wo': Wo, 'bo': bo, 'gamma': gamma, 'beta': beta}
    _L3_gnn_all = _L3_gnn_setup()
    _L3_gnn_in = {k: v for k, v in _L3_gnn_all.items() if k in ('Wq', 'Wk', 'Wv', 'Wo', 'bo', 'gamma', 'beta')}
    del _L3_gnn_all
    return {'x': x, 'adj': adj, 'L0_gnn_ln1_g': _L0_gnn_in['ln1_g'], 'L0_gnn_ln1_b': _L0_gnn_in['ln1_b'], 'L0_gnn_ln2_g': _L0_gnn_in['ln2_g'], 'L0_gnn_ln2_b': _L0_gnn_in['ln2_b'], 'L0_gnn_wq': _L0_gnn_in['wq'], 'L0_gnn_bq': _L0_gnn_in['bq'], 'L0_gnn_wk': _L0_gnn_in['wk'], 'L0_gnn_bk': _L0_gnn_in['bk'], 'L0_gnn_wv': _L0_gnn_in['wv'], 'L0_gnn_bv': _L0_gnn_in['bv'], 'L0_gnn_wo': _L0_gnn_in['wo'], 'L0_gnn_bo': _L0_gnn_in['bo'], 'L0_gnn_w1': _L0_gnn_in['w1'], 'L0_gnn_b1': _L0_gnn_in['b1'], 'L0_gnn_w2': _L0_gnn_in['w2'], 'L0_gnn_b2': _L0_gnn_in['b2'], 'L1_gnn_Wq': _L1_gnn_in['Wq'], 'L1_gnn_bq': _L1_gnn_in['bq'], 'L1_gnn_Wk': _L1_gnn_in['Wk'], 'L1_gnn_bk': _L1_gnn_in['bk'], 'L1_gnn_Wc': _L1_gnn_in['Wc'], 'L1_gnn_ln_g': _L1_gnn_in['ln_g'], 'L1_gnn_ln_b': _L1_gnn_in['ln_b'], 'L2_gnn_Wq': _L2_gnn_in['Wq'], 'L2_gnn_bq': _L2_gnn_in['bq'], 'L2_gnn_Wk': _L2_gnn_in['Wk'], 'L2_gnn_bk': _L2_gnn_in['bk'], 'L2_gnn_Wv': _L2_gnn_in['Wv'], 'L2_gnn_bv': _L2_gnn_in['bv'], 'L2_gnn_Wo': _L2_gnn_in['Wo'], 'L2_gnn_bo': _L2_gnn_in['bo'], 'L2_gnn_gamma': _L2_gnn_in['gamma'], 'L2_gnn_beta': _L2_gnn_in['beta'], 'L3_gnn_Wq': _L3_gnn_in['Wq'], 'L3_gnn_Wk': _L3_gnn_in['Wk'], 'L3_gnn_Wv': _L3_gnn_in['Wv'], 'L3_gnn_Wo': _L3_gnn_in['Wo'], 'L3_gnn_bo': _L3_gnn_in['bo'], 'L3_gnn_gamma': _L3_gnn_in['gamma'], 'L3_gnn_beta': _L3_gnn_in['beta']}

def reference(x, adj, L0_gnn_ln1_g, L0_gnn_ln1_b, L0_gnn_ln2_g, L0_gnn_ln2_b, L0_gnn_wq, L0_gnn_bq, L0_gnn_wk, L0_gnn_bk, L0_gnn_wv, L0_gnn_bv, L0_gnn_wo, L0_gnn_bo, L0_gnn_w1, L0_gnn_b1, L0_gnn_w2, L0_gnn_b2, L1_gnn_Wq, L1_gnn_bq, L1_gnn_Wk, L1_gnn_bk, L1_gnn_Wc, L1_gnn_ln_g, L1_gnn_ln_b, L2_gnn_Wq, L2_gnn_bq, L2_gnn_Wk, L2_gnn_bk, L2_gnn_Wv, L2_gnn_bv, L2_gnn_Wo, L2_gnn_bo, L2_gnn_gamma, L2_gnn_beta, L3_gnn_Wq, L3_gnn_Wk, L3_gnn_Wv, L3_gnn_Wo, L3_gnn_bo, L3_gnn_gamma, L3_gnn_beta):
    import jax
    import jax.numpy as jnp

    def _L0_gnn_ref(x, adj_matrix, edge_attr_matrix, ln1_g, ln1_b, ln2_g, ln2_b, wq, bq, wk, bk, wv, bv, wo, bo, w1, b1, w2, b2):
        import jax, jax.numpy as jnp
        import numpy as np
        B, S, D, H = (2, 1024, 256, 8)
        HD = D // H
        EPS = 1e-05

        def _ln(x, g, b):
            mu = jnp.mean(x, axis=-1, keepdims=True)
            var = jnp.mean((x - mu) ** 2, axis=-1, keepdims=True)
            return (x - mu) * jax.lax.rsqrt(var + EPS) * g + b
        b, s, d = x.shape
        residual = x
        nx = _ln(x, ln1_g, ln1_b)
        q = (nx @ wq + bq).reshape(b, s, H, HD).transpose(0, 2, 1, 3)
        k = (nx @ wk + bk).reshape(b, s, H, HD).transpose(0, 2, 1, 3)
        v = (nx @ wv + bv).reshape(b, s, H, HD).transpose(0, 2, 1, 3)
        adjf = adj_matrix.astype(jnp.float32)
        bias = jnp.where(adj_matrix > 0, 0.1 * edge_attr_matrix * adjf, -jnp.inf)[:, None]
        scores = jnp.einsum('bhqd,bhkd->bhqk', q, k) / np.sqrt(HD) + bias
        attn = jax.nn.softmax(scores, axis=-1)
        out = jnp.einsum('bhqk,bhkd->bhqd', attn, v)
        out = out.transpose(0, 2, 1, 3).reshape(b, s, d)
        x1 = residual + (out @ wo + bo)
        n2 = _ln(x1, ln2_g, ln2_b)
        mlp = jax.nn.gelu(n2 @ w1 + b1, approximate=False) @ w2 + b2
        return x1 + mlp

    def _L1_gnn_ref(node_fts, rel_edges, Wq, bq, Wk, bk, Wc, ln_g, ln_b):
        import jax, jax.numpy as jnp
        import numpy as np
        B, N, E, FF, L = (8, 1024, 256, 128, 2)
        LN_EPS = 1e-05
        SCALE = float(np.sqrt(FF))

        def layer_norm(x, g, b):
            m = jnp.mean(x, axis=-1, keepdims=True)
            v = jnp.mean(jnp.square(x - m), axis=-1, keepdims=True)
            return (x - m) * jax.lax.rsqrt(v + LN_EPS) * g + b
        x = node_fts
        mask = rel_edges == 0
        for k in range(L):
            q = jnp.einsum('bnd,fd->bnf', x, Wq[k]) + bq[k]
            kk = jnp.einsum('bnd,fd->bnf', x, Wk[k]) + bk[k]
            scores = jnp.einsum('bof,bif->boi', q, kk) / SCALE
            scores = jnp.where(mask, -10000000000.0, scores)
            attn = jax.nn.softmax(scores, axis=2)
            attn = jnp.where(mask, 0.0, attn)
            ctx = jnp.einsum('boi,bid->bod', attn, x)
            ctx = jnp.einsum('bnd,ed->bne', ctx, Wc[k])
            x = layer_norm(x + ctx, ln_g[k], ln_b[k])
        return x

    def _L2_gnn_ref(x, adj, Wq, bq, Wk, bk, Wv, bv, Wo, bo, gamma, beta):
        import jax, jax.numpy as jnp
        import numpy as np
        B, N, D, H = (4, 1024, 256, 8)
        HD = D // H
        EPS = 1e-05
        b, n, d = x.shape
        scale = 1.0 / np.sqrt(HD).astype(np.float32)
        q = (x @ Wq + bq).reshape(b, n, H, HD)
        k = (x @ Wk + bk).reshape(b, n, H, HD)
        v = (x @ Wv + bv).reshape(b, n, H, HD)
        scores = jnp.einsum('bnhd,bmhd->bhnm', q, k) * scale
        mask = (adj == 0)[:, None, :, :]
        scores = jnp.where(mask, jnp.float32(-jnp.inf), scores)
        attn = jax.nn.softmax(scores, axis=-1)
        h = jnp.einsum('bhnm,bmhd->bnhd', attn, v).reshape(b, n, d)
        h = h @ Wo + bo
        y = h + x
        mu = jnp.mean(y, axis=-1, keepdims=True)
        var = jnp.mean(jnp.square(y - mu), axis=-1, keepdims=True)
        return (y - mu) * jax.lax.rsqrt(var + EPS) * gamma + beta

    def _L3_gnn_ref(x, adj, Wq, Wk, Wv, Wo, bo, gamma, beta):
        import jax, jax.numpy as jnp
        import numpy as np
        import math
        D = 256
        B, L = (8, 1024)
        EPS = 1e-05

        def layer_norm(y, gamma, beta):
            mu = jnp.mean(y, axis=-1, keepdims=True)
            var = jnp.mean(jnp.square(y - mu), axis=-1, keepdims=True)
            return (y - mu) * jax.lax.rsqrt(var + EPS) * gamma + beta
        d_out = Wq.shape[1]
        scale = 1.0 / math.sqrt(d_out)
        Q = x @ Wq
        K = x @ Wk
        V = x @ Wv
        sc = jnp.einsum('bld,bmd->blm', Q, K) * scale
        mask = adj == 0
        sc = jnp.where(mask, -jnp.inf, sc)
        all_inf = jnp.all(mask, axis=-1, keepdims=True)
        sc = jnp.where(all_inf, 0.0, sc)
        w = jax.nn.softmax(sc, axis=-1)
        out = jnp.einsum('blm,bmd->bld', w, V)
        y = x + out @ Wo + bo
        return layer_norm(y, gamma, beta)
    x = _L0_gnn_ref(x, adj, adj, L0_gnn_ln1_g, L0_gnn_ln1_b, L0_gnn_ln2_g, L0_gnn_ln2_b, L0_gnn_wq, L0_gnn_bq, L0_gnn_wk, L0_gnn_bk, L0_gnn_wv, L0_gnn_bv, L0_gnn_wo, L0_gnn_bo, L0_gnn_w1, L0_gnn_b1, L0_gnn_w2, L0_gnn_b2)
    x = _L1_gnn_ref(x, adj, L1_gnn_Wq, L1_gnn_bq, L1_gnn_Wk, L1_gnn_bk, L1_gnn_Wc, L1_gnn_ln_g, L1_gnn_ln_b)
    x = _L2_gnn_ref(x, adj, L2_gnn_Wq, L2_gnn_bq, L2_gnn_Wk, L2_gnn_bk, L2_gnn_Wv, L2_gnn_bv, L2_gnn_Wo, L2_gnn_bo, L2_gnn_gamma, L2_gnn_beta)
    x = _L3_gnn_ref(x, adj, L3_gnn_Wq, L3_gnn_Wk, L3_gnn_Wv, L3_gnn_Wo, L3_gnn_bo, L3_gnn_gamma, L3_gnn_beta)
    return x

_drawn_inputs = setup_inputs


def setup_inputs(seed=0):
    import zlib

    import numpy as np

    out = dict(_drawn_inputs(seed))
    spreads = {'L0_gnn_ln1_g': (1.0, 0.2),
     'L0_gnn_ln1_b': (0.0, 0.1),
     'L0_gnn_ln2_g': (1.0, 0.2),
     'L0_gnn_ln2_b': (0.0, 0.1),
     'L0_gnn_bq': (0.0, 0.1),
     'L0_gnn_bk': (0.0, 0.8),
     'L0_gnn_bv': (0.0, 0.1),
     'L0_gnn_bo': (0.0, 0.1),
     'L0_gnn_b1': (0.0, 0.1),
     'L0_gnn_b2': (0.0, 0.1),
     'L1_gnn_bq': (0.0, 0.8),
     'L1_gnn_bk': (0.0, 0.8),
     'L1_gnn_ln_g': (1.0, 0.2),
     'L1_gnn_ln_b': (0.0, 0.1),
     'L2_gnn_bq': (0.0, 0.8),
     'L2_gnn_bk': (0.0, 0.8),
     'L2_gnn_bv': (0.0, 0.1),
     'L2_gnn_bo': (0.0, 0.1),
     'L2_gnn_gamma': (1.0, 0.2),
     'L2_gnn_beta': (0.0, 0.1),
     'L3_gnn_bo': (0.0, 0.1),
     'L3_gnn_gamma': (1.0, 0.2),
     'L3_gnn_beta': (0.0, 0.1)}
    factors = {}
    for name, (base, spread) in spreads.items():
        noise = np.random.default_rng([zlib.crc32(name.encode()), seed]).standard_normal(out[name].shape)
        drawn = base * np.exp(spread * noise) if base else spread * noise
        out[name] = jnp.asarray(drawn.astype(out[name].dtype))
    for name, factor in factors.items():
        out[name] = (out[name] * factor).astype(out[name].dtype)
    return out
```

```python
from contextlib import ExitStack

import numpy as np

import concourse.bass as bass
from concourse import mybir

F32 = mybir.dt.float32
F32R = mybir.dt.float32r
F16 = mybir.dt.float16
BF16 = mybir.dt.bfloat16
I32 = mybir.dt.int32
ALU = mybir.AluOpType
ACT = mybir.ActivationFunctionType
AX = mybir.AxisListType

P = 128
D = 256
C = D // P
B = 4
R = B * P
H = 8
HD = D // H
HC = P // HD
FF = 4 * D
FT = FF // P
CH = 2
NCH = FT // CH
DK = 128
EPS = 1e-5
MASKED = -1e30
STREAMS = 1
SLOTS = 4


class Signal:

    START = 1

    def __init__(self, sem, keys, unit=1):
        self.sem, self.keys, self.unit = sem, list(keys), unit
        self.rank = {k: n for n, k in enumerate(self.keys)}
        assert len(self.rank) == len(self.keys)

    def at(self, it, key):
        return self.sem, it * (len(self.keys) * self.unit) + ((self.rank[key] + 1) * self.unit + self.START)

    def before(self, it):
        return self.sem, it * (len(self.keys) * self.unit) + self.START


class Chain:

    def __init__(self, engine, sem, it, per_step):
        self.engine, self.sem, self.it, self.per_step, self.n = engine, sem, it, per_step, 0

    def link(self, instruction):
        instruction.then_inc(self.sem, 1)
        self.n += 1
        self.engine.wait_ge(self.sem, self.it * self.per_step + self.n)

    def end(self):
        assert self.n == self.per_step, (self.n, self.per_step)


def plan():
    stages = []
    for name, layer in (
        [("load", 0), ("norm_in", 0), ("to_T", "0"), ("qkv", 0), ("heads", 0), ("to_T", "0a"), ("out_proj", 0),
         ("norm_mid", 0), ("to_T", "0m"), ("mlp", 0)]
        + [(n, l) for l in (1, 2) for n in ("to_T", "qk1", "one_head", "out_proj", "norm_out")]
        + [("to_T", 3), ("qkv", 3), ("heads", 3), ("to_T", "3a"), ("out_proj", 3), ("norm_out", 3)]
        + [(n, 4) for n in ("to_T", "qk1", "one_head", "out_proj", "norm_out", "store")]
    ):
        stages += [(name, s, layer) for s in range(STREAMS)]
    return stages


def units_of(stage, s, layer):
    if stage == "to_T":
        return [("T", s, layer)]
    if stage == "qkv":
        return [(u, s, layer) for u in "qkv"]
    if stage == "heads":
        out = []
        for i in range(B + 2):
            out += [("S", s, layer, i)] * (i < B) + [("P", s, layer, i - 1)] * (1 <= i <= B) + [("O", s, layer, i - 2)] * (i >= 2)
        return out
    if stage == "mlp":
        return [("h", s, layer, 0), ("h", s, layer, 1), ("y", s, layer), ("h", s, layer, 2), ("h", s, layer, 3)]
    if stage == "qk1":
        return [("qk", s, layer)]
    if stage == "one_head":
        return [("S", s, layer), ("P", s, layer), ("X", s, layer)]
    if stage == "out_proj":
        return [("o", s, layer)]
    return []


def mk_kernel(nc, steps, t, out):
    scale_hd = float(1.0 / np.sqrt(HD))
    scale_dk = float(1.0 / np.sqrt(DK))
    scale_d = float(1.0 / np.sqrt(D))
    ctx = ExitStack()
    with ctx:
        def sb(name, shape, dt):
            return ctx.enter_context(nc.sbuf_tensor(name, shape, dt))

        def sem(name):
            return ctx.enter_context(nc.semaphore(name))

        jobs = [
            ("q0", "L0_gnn_wq", C, D, "ln1_gs"), ("k0", "L0_gnn_wk", C, D, "ln1_g"), ("v0", "L0_gnn_wv", C, D, "ln1_g"),
            ("o0", "L0_gnn_wo", C, D, None), ("w1", "L0_gnn_w1", C, FF, "ln2_g"), ("w2", "L0_gnn_w2", FT, D, None),
            ("q1", "L1_gnn_WqT0", C, DK, scale_dk), ("k1", "L1_gnn_WkT0", C, DK, None), ("o1", "L1_gnn_WcT0", C, D, None),
            ("q2", "L1_gnn_WqT1", C, DK, scale_dk), ("k2", "L1_gnn_WkT1", C, DK, None), ("o2", "L1_gnn_WcT1", C, D, None),
            ("q3", "L2_gnn_Wq", C, D, scale_hd), ("k3", "L2_gnn_Wk", C, D, None), ("v3", "L2_gnn_Wv", C, D, None),
            ("o3", "L2_gnn_Wo", C, D, None),
            ("q4", ("L3_gnn_WqT", "L3_gnn_WkT"), C, D, scale_d), ("o4", ("L3_gnn_WvT", "L3_gnn_Wo"), C, D, None),
        ]
        w = {j[0]: sb(f"w_{j[0]}", [P, 2, j[2], j[3]], F32R) for j in jobs}

        cols = {}
        for name, src, n in (
            ("ln1_g", "L0_gnn_ln1_g", C), ("ln1_b", "L0_gnn_ln1_b", C), ("ln2_g", "L0_gnn_ln2_g", C),
            ("ln2_b", "L0_gnn_ln2_b", C), ("bq0", "L0_gnn_bq", C), ("bk0", "L0_gnn_bk", C), ("bv0", "L0_gnn_bv", C),
            ("b1", "L0_gnn_b1", FT), ("bq1", "L1_gnn_bq0", 1), ("bk1", "L1_gnn_bk0", 1), ("bq2", "L1_gnn_bq1", 1),
            ("bk2", "L1_gnn_bk1", 1), ("bq3", "L2_gnn_bq", C), ("bk3", "L2_gnn_bk", C), ("bv3", "L2_gnn_bv", C),
        ):
            cols[name] = (sb(f"c_{name}", [P, n], F32), src)
        ln1_gs = sb("ln1_gs", [P, C], F32)
        rows = {}
        for name, src in (
            ("bo0", "L0_gnn_bo"), ("b2", "L0_gnn_b2"), ("bo3", "L2_gnn_bo"), ("bo4", "L3_gnn_bo"),
            ("g1", "L1_gnn_ln_g0"), ("b_1", "L1_gnn_ln_b0"), ("g2", "L1_gnn_ln_g1"), ("b_2", "L1_gnn_ln_b1"),
            ("g3", "L2_gnn_gamma"), ("b_3", "L2_gnn_beta"), ("g4", "L3_gnn_gamma"), ("b_4", "L3_gnn_beta"),
        ):
            rows[name] = (sb(f"r_{name}", [P, D], F32), src)
        ident = sb("ident", [P, P], F32)
        ones = sb("ones", [P, P], F32)
        bv_wide = sb("bv_wide", [P, C, P], F32)
        started = sb("started", [P, 32], F32)
        minus_half = sb("minus_half", [P, B], F32)

        x = [sb(f"x{s}", [P, B, D], F32) for s in range(STREAMS)]
        xn = [sb(f"xn{s}", [P, B, D], F32) for s in range(STREAMS)]
        xT = [sb(f"xT{s}", [P, 2, C, R], F32R) for s in range(STREAMS)]
        qT = [sb(f"qT{s}", [P, 2, C, R], F32R) for s in range(STREAMS)]
        v = [sb(f"v{s}", [P, 3, B, D], BF16) for s in range(STREAMS)]
        adj = [sb(f"adj{s}", [P, B, P], I32) for s in range(STREAMS)]
        bias = [sb(f"bias{s}", [P, B, P], F32) for s in range(STREAMS)]
        kT = sb("kT", [P, 2, C, R], F32)
        kD = [sb(f"kD{n}", [P, 2, C, HC, P], F32R) for n in range(2)]
        e = sb("e", [P, 2, H, P], F32)
        p16 = [sb(f"p16_{n}", [P, 2, H, P], F16) for n in range(2)]
        hT = [sb(f"hT{n}", [P, 2, CH, R], F32R) for n in range(2)]
        stats = sb("stats", [P, B, 6], F32)
        mean = sb("mean", [P, B], F32)
        gap = sb("gap", [P, B], F32)
        var = sb("var", [P, B], F32)
        rstd = sb("rstd", [P, B], F32)
        neg_max = sb("neg_max", [P, 2, H], F32)
        total = sb("total", [P, 2, H], F32)
        rinv = sb("rinv", [P, 2, H], F32)
        xT_full = kT[:, 0]

        slot = [ctx.enter_context(nc.psum_tensor(f"slot{n}", [P, 2, 512], F32)) for n in range(SLOTS)]

        stages = plan()
        units = [u for st in stages for u in units_of(*st)]
        nth = {u: n for n, u in enumerate(units)}
        assert len(units) % SLOTS == 0 and len(nth) == len(units)

        def psum(u):
            return slot[nth[u] % SLOTS]

        def keyed(stage, *more):
            return [(s, l, *m) for n, s, l in stages if n == stage for m in (more or [()])]

        eight = [(s, l, b) for n, s, l in stages if n == "heads" for b in range(B)]
        attn = [(s, l, b) for n, s, l in stages if n in ("heads", "one_head") for b in (range(B) if n == "heads" else (0,))]
        filled = Signal(sem("filled"), [u for u in units if u[0] != "y"])
        taken = [Signal(sem(f"taken{n}"), units[n::SLOTS]) for n in range(SLOTS)]
        half_units = [u for u in units if u[0] in ("T", "q", "k", "v", "P", "h", "X") and not (u[0] == "P" and len(u) == 3)]
        hi_taken = Signal(sem("hi_taken"), half_units)
        full_taken = Signal(sem("full_taken"), [u for u in units if u[0] == "T" and u[2] == 4])
        y_done = Signal(sem("y_done"), keyed("mlp"))
        x_in = Signal(sem("x_in"), keyed("load"), 16)
        adj_in = Signal(sem("adj_in"), keyed("load"), 16)
        stored = Signal(sem("stored"), keyed("store"), 16)
        kD_in = [Signal(sem(f"kD_in{n}"), [k for k in eight if k[2] % 2 == n], 16 * HC) for n in range(2)]
        norms = [(s, l) for n, s, l in stages if n in ("norm_in", "norm_mid", "norm_out")]
        norm_key = {("norm_in", 0): 0, ("norm_mid", 0): "mid"}
        norms = [(s, norm_key.get((n, l), l)) for n, s, l in stages if n in ("norm_in", "norm_mid", "norm_out")]
        var_ready = Signal(sem("var_ready"), norms)
        rstd_ready = Signal(sem("rstd_ready"), norms)
        rows_ready = Signal(sem("rows_ready"), norms)
        b_added = Signal(sem("b_added"), [(s, k) for n, s, l in stages for k in
                                          ({("norm_in", 0): (0,), ("norm_mid", 0): ("mid",), ("qkv", 3): (3,), ("one_head", 4): (4,)}.get((n, l), ()))])
        scores_ready = Signal(sem("scores_ready"), attn)
        exp_ready = Signal(sem("exp_ready"), attn)
        p_ready = Signal(sem("p_ready"), keyed("one_head"))
        v_ready = Signal(sem("v_ready"), keyed("qkv"))
        h_ready = Signal(sem("h_ready"), [(s, j) for n, s, l in stages if n == "mlp" for j in range(NCH)])
        act_step, dve_step, pool_step = sem("act_step"), sem("dve_step"), sem("pool_step")
        signals = [filled, *taken, hi_taken, full_taken, y_done, x_in, adj_in, stored, *kD_in, var_ready, rstd_ready, rows_ready,
                   b_added, scores_ready, exp_ready, p_ready, v_ready, h_ready]
        par_in, one_made = sem("par_in"), sem("const_made")
        w_in = [sem(f"w_in{n}") for n in range(2)]
        w_mm, w_hi, w_lo, w_col, w_bias = sem("w_mm"), sem("w_hi"), sem("w_lo"), sem("w_col"), sem("w_bias")
        dve_pro = sem("dve_pro")
        n_par = len(cols) + len(rows)
        JN = len(jobs)

        def staging(j):
            base = kT[:].rearrange("p a c r -> p (a c r)") if j % 2 == 0 else e[:].rearrange("p a h k -> p (a h k)")
            _, _, kt, n, _ = jobs[j]
            return base[:, 0:kt * n].rearrange("p (k n) -> p k n", k=kt)

        def staging2(j):
            base = kT[:].rearrange("p a c r -> p (a c r)") if j % 2 == 0 else e[:].rearrange("p a h k -> p (a h k)")
            return base[:, C * D:2 * C * D].rearrange("p (k n) -> p k n", k=C)

        MM_JOBS = [j for j, jb in enumerate(jobs) if jb[0] in ("q0", "k0", "v0", "o0", "w1", "o3", "q4", "o4")]
        mm_rank = {j: n for n, j in enumerate(MM_JOBS)}

        def heads(ap):
            return ap.rearrange("p (h k) -> p h k", k=P)

        block = ctx.enter_context(nc.Block())

        @block.sync
        def _(sp):
            for name, (dst, src) in cols.items():
                sp.dma_start(dst[:, :], t[src + "_col"]).then_inc(par_in, 16)
            for name, (dst, src) in rows.items():
                sp.dma_start(dst[:, :], t[src].unsqueeze(0).broadcast_to([P, D])).then_inc(par_in, 16)
            for j, (name, src, kt, n, _) in enumerate(jobs):
                if j >= 2:
                    sp.wait_ge(w_lo, j - 1)
                    sp.wait_ge(w_hi, j - 1)
                if isinstance(src, tuple):
                    sp.dma_start(staging(j), t[src[0]].rearrange("(k p) n -> p k n", p=P)).then_inc(w_in[j % 2], 16)
                    sp.dma_start(staging2(j), t[src[1]].rearrange("(k p) n -> p k n", p=P)).then_inc(w_in[j % 2], 16)
                else:
                    sp.dma_start(staging(j), t[src].rearrange("(k p) n -> p k n", p=P)).then_inc(w_in[j % 2], 16)
            x_v = t["x"].rearrange("(i b) n f -> i n b f", b=B)
            adj_v = t["adj"].rearrange("(i b) n m -> i n b m", b=B)
            out_v = out.rearrange("(i b) n f -> i n b f", b=B)
            sp.wait_ge(w_lo, JN)
            with sp.Fori(0, steps) as it:
                for stage, s, l in stages:
                    if stage == "load":
                        sp.wait_ge(*stored.before(it))
                        sp.dma_start(x[s][:, :, :], x_v[it * STREAMS + s]).then_inc(x_in.sem, 16)
                        sp.dma_start(adj[s][:, :, :], adj_v[it * STREAMS + s]).then_inc(adj_in.sem, 16)
                    elif stage == "heads":
                        sp.wait_ge(*taken[nth["k", s, l] % SLOTS].at(it, ("k", s, l)))
                        for b in range(B):
                            if b >= 2:
                                sp.wait_ge(*filled.at(it, ("S", s, l, b - 2)))
                            for h in range(HC):
                                q = slice(h * HD, (h + 1) * HD)
                                sp.dma_start(
                                    kD[b % 2][q, :, :, h, :].bitcast(F32).rearrange("p a c k -> p (a c) k"),
                                    kT[q, :, :, b * P:(b + 1) * P].rearrange("p a c k -> p (a c) k"),
                                ).then_inc(kD_in[b % 2].sem, 16)
                    elif stage == "store":
                        sp.wait_ge(*rows_ready.at(it, (s, 4)))
                        sp.dma_start(out_v[it * STREAMS + s], x[s][:, :, :]).then_inc(stored.sem, 16)
            sp.wait_ge(*stored.before(steps))

        @block.gpsimd
        def _(pool):
            nc.gpsimd.memset(ident[:, :], 0.0).then_inc(pool_step, 1)
            pool.wait_ge(pool_step, 1)
            nc.gpsimd.affine_select(out=ident[:, :], in_=ident[:, :], compare_op=ALU.not_equal, fill=1.0, base=0,
                                    pattern=[[-1, P]], channel_multiplier=1).then_inc(one_made, 1)
            nc.gpsimd.memset(ones[:, :], 1.0).then_inc(one_made, 1)
            nc.gpsimd.memset(minus_half[:, :], -0.5).then_inc(one_made, 1)
            for n in range(2):
                nc.gpsimd.memset(kD[n][:].bitcast(F32), 0.0).then_inc(one_made, 1)
            for n, signal in enumerate(signals):
                nc.gpsimd.memset(started[:, n:n + 1], 0.0).then_inc(signal.sem, Signal.START)
            pool.wait_ge(one_made, 5)
            pool.wait_ge(par_in, 16 * n_par)
            pool.wait_ge(w_bias, 2)

            def add_rows(it, s, key, row):
                nc.gpsimd.tensor_tensor(x[s][:, :, :], x[s][:, :, :],
                                        rows[row][0][:, :].unsqueeze(1).broadcast_to([P, B, D]), ALU.add).then_inc(b_added.sem, 1)

            with pool.Fori(0, steps) as it:
                for stage, s, l in stages:
                    key = norm_key.get((stage, l), l)
                    if stage in ("norm_in", "norm_mid", "norm_out"):
                        pool.wait_ge(*var_ready.at(it, (s, key)))
                        nc.gpsimd.tensor_tensor(rstd[:, :], var[:, :], minus_half[:, :], ALU.pow).then_inc(rstd_ready.sem, 1)
                    if stage in ("norm_in", "norm_mid"):
                        pool.wait_ge(*rows_ready.at(it, (s, key)))
                        add_rows(it, s, key, "bo0" if key == 0 else "b2")
                    if stage == "qkv" and l == 3:
                        pool.wait_ge(*filled.at(it, ("T", s, 3)))
                        add_rows(it, s, 3, "bo3")
                    if stage == "one_head" and l == 4:
                        pool.wait_ge(*filled.at(it, ("X", s, 4)))
                        add_rows(it, s, 4, "bo4")

        @block.tensor
        def _(pe):
            mm = nc.tensor.matmul

            def three(dst, a, b_, first, last, **kw):
                mm(dst, a(1), b_(0), start=first, stop=False, **kw)
                mm(dst, a(0), b_(1), start=False, stop=False, **kw)
                return mm(dst, a(0), b_(0), start=False, stop=last, **kw)

            pe.wait_ge(one_made, 5)
            pe.wait_ge(par_in, 16 * n_par)
            w_loads = [0, 0]
            for j, (name, src, kt, n, _) in enumerate(jobs):
                w_loads[j % 2] += 16 * (2 if isinstance(src, tuple) else 1)
                if j not in mm_rank:
                    continue
                pe.wait_ge(w_in[j % 2], w_loads[j % 2])
                if mm_rank[j] >= SLOTS:
                    pe.wait_ge(w_lo, MM_JOBS[mm_rank[j] - SLOTS] + 1)
                    pe.wait_ge(w_hi, MM_JOBS[mm_rank[j] - SLOTS] + 1)
                ps = slot[mm_rank[j] % SLOTS]
                st = staging(j)
                if name in ("q0", "k0", "v0", "w1"):
                    b_col = cols["ln2_b" if name == "w1" else "ln1_b"][0]
                    for m in range(n // P):
                        for c in range(C):
                            last = mm(ps[:, 0, m:m + 1], st[:, c, m * P:(m + 1) * P], b_col[:, c:c + 1],
                                      start=c == 0, stop=c == C - 1)
                elif name in ("o0", "o3"):
                    pe.wait_ge(w_col, 2 if name == "o0" else 3)
                    for c in range(C):
                        last = mm(ps[:, 0, 0:D], bv_wide[:, c, :], st[:, c, :], start=c == 0, stop=c == C - 1)
                else:
                    st2 = staging2(j)
                    for m in range(C):
                        for c in range(C):
                            last = mm(ps[:, m, 0:D], st[:, c, m * P:(m + 1) * P], st2[:, c, :], start=c == 0, stop=c == C - 1)
                last.then_inc(w_mm, 1)
            pe.wait_ge(w_lo, JN)

            def enter(it, u):
                n = nth[u]
                if n >= SLOTS:
                    pe.wait_ge(*taken[n % SLOTS].at(it, units[n - SLOTS]))
                else:
                    pe.wait_ge(*taken[n % SLOTS].before(it))

            def took(it, u):
                pe.wait_ge(*taken[nth[u] % SLOTS].at(it, u))

            with pe.Fori(0, steps) as it:
                for stage, s, l in stages:
                    X = xT[s]
                    if stage == "to_T":
                        u = ("T", s, l)
                        src = x[s]
                        if l in ("0", "0m"):
                            pe.wait_ge(*rows_ready.at(it, (s, 0 if l == "0" else "mid")))
                            src = xn[s]
                        elif l in ("0a", "3a"):
                            ly = int(l[0])
                            took(it, ("O", s, ly, B - 1))
                            src = xn[s]
                        elif l == 1:
                            took(it, ("y", s, 0))
                        else:
                            pe.wait_ge(*rows_ready.at(it, (s, l - 1)))
                        enter(it, u)
                        for c in range(C):
                            for b in range(B):
                                last = nc.tensor.transpose(psum(u)[:, c, b * P:(b + 1) * P], src[:, b, c * P:(c + 1) * P], ident[:, :])
                        last.then_inc(filled.sem, 1)
                    elif stage == "qkv":
                        took(it, ("T", s, "0" if l == 0 else l))
                        for name in "qk":
                            u = (name, s, l)
                            enter(it, u)
                            W = w[f"{name}{l}"]
                            for m in range(C):
                                for c in range(C):
                                    last = three(psum(u)[:, m, :], lambda p: W[:, p, c, m * P:(m + 1) * P],
                                                 lambda p: X[:, p, c, :], c == 0, c == C - 1)
                            last.then_inc(filled.sem, 1)
                        u = ("v", s, l)
                        enter(it, u)
                        W = w[f"v{l}"]
                        for b in range(B):
                            for c in range(C):
                                last = three(psum(u)[:, b // 2, b % 2 * D:(b % 2 + 1) * D], lambda p: X[:, p, c, b * P:(b + 1) * P],
                                             lambda p: W[:, p, c, :], c == 0, c == C - 1)
                        last.then_inc(filled.sem, 1)
                    elif stage == "heads":
                        took(it, ("q", s, l))
                        for u in units_of(stage, s, l):
                            b = u[3]
                            if u[0] == "S":
                                pe.wait_ge(*kD_in[b % 2].at(it, (s, l, b)))
                                enter(it, u)
                                for c in range(C):
                                    last = three(psum(u)[:, c, :], lambda p: qT[s][:, p, c, b * P:(b + 1) * P],
                                                 lambda p: kD[b % 2][:, p, c].rearrange("p h k -> p (h k)"), True, True)
                                last.then_inc(filled.sem, 1)
                            elif u[0] == "P":
                                pe.wait_ge(*exp_ready.at(it, (s, l, b)))
                                enter(it, u)
                                for h in range(H):
                                    last = nc.tensor.transpose(psum(u)[:, h // HC, h % HC * P:(h % HC + 1) * P], e[:, b % 2, h, :], ident[:, :])
                                last.then_inc(filled.sem, 1)
                            else:
                                if b == 0:
                                    pe.wait_ge(*v_ready.at(it, (s, l)))
                                took(it, ("P", s, l, b))
                                enter(it, u)
                                for h in range(H):
                                    dst = psum(u)[:, 0, h * HD:(h + 1) * HD]
                                    terms = [(1, 1), (1, 0), (0, 2), (0, 1), (0, 0)]
                                    for n, (pp, vp) in enumerate(terms):
                                        last = mm(dst, p16[b % 2][:, pp, h, :], v[s][:, vp, b, h * HD:(h + 1) * HD],
                                                  start=n == 0, stop=n == len(terms) - 1)
                                last.then_inc(filled.sem, 1)
                    elif stage == "out_proj":
                        u = ("o", s, l)
                        took(it, ("T", s, f"{l}a") if l in (0, 3) else ("X", s, l))
                        enter(it, u)
                        W = w[f"o{l}"]
                        for b in range(B):
                            for c in range(C):
                                last = three(psum(u)[:, b // 2, b % 2 * D:(b % 2 + 1) * D], lambda p: X[:, p, c, b * P:(b + 1) * P],
                                             lambda p: W[:, p, c, :], c == 0, c == C - 1)
                        last.then_inc(filled.sem, 1)
                    elif stage == "mlp":
                        took(it, ("T", s, "0m"))
                        y = ("y", s, l)

                        def hidden(j):
                            u = ("h", s, l, j)
                            enter(it, u)
                            for i in range(CH):
                                f = (j * CH + i) * P
                                for c in range(C):
                                    last = three(psum(u)[:, i, :], lambda p: w["w1"][:, p, c, f:f + P], lambda p: X[:, p, c, :],
                                                 c == 0, c == C - 1)
                            last.then_inc(filled.sem, 1)

                        def project(j):
                            pe.wait_ge(*h_ready.at(it, (s, j)))
                            if j == 0:
                                enter(it, y)
                            for b in range(B):
                                for i in range(CH):
                                    last = three(psum(y)[:, b // 2, b % 2 * D:(b % 2 + 1) * D],
                                                 lambda p: hT[j % 2][:, p, i, b * P:(b + 1) * P],
                                                 lambda p: w["w2"][:, p, j * CH + i, :], j == 0 and i == 0 and b % 2 == 0,
                                                 j == NCH - 1 and i == CH - 1, skip_group_check=True)
                            return last

                        hidden(0)
                        hidden(1)
                        project(0)
                        hidden(2)
                        project(1)
                        hidden(3)
                        project(2)
                        project(3).then_inc(y_done.sem, 1)
                    elif stage == "qk1":
                        u = ("qk", s, l)
                        took(it, ("T", s, l))
                        enter(it, u)
                        if l == 4:
                            outs = [(w["q4"], m * P, m) for m in range(C)]
                        else:
                            outs = [(w[f"q{l}"], 0, 0), (w[f"k{l}"], 0, 1)]
                        for W, f, m in outs:
                            for c in range(C):
                                last = three(psum(u)[:, m, :], lambda p: W[:, p, c, f:f + P], lambda p: X[:, p, c, :], c == 0, c == C - 1)
                        last.then_inc(filled.sem, 1)
                    elif stage == "one_head":
                        u = ("S", s, l)
                        took(it, ("qk", s, l))
                        if l == 4:
                            pe.wait_ge(*full_taken.at(it, ("T", s, 4)))
                        enter(it, u)
                        q = xn[s][:].rearrange("p b d -> p (b d)")
                        for b in range(B):
                            g = slice(b * P, (b + 1) * P)
                            pairs = [(q[:, 0:R][:, g], q[:, R:2 * R][:, g])] if l != 4 else \
                                    [(q[:, c * R:(c + 1) * R][:, g], xT_full[:, c, g]) for c in range(C)]
                            for n, (a, k) in enumerate(pairs):
                                last = mm(psum(u)[:, 0, g], a, k, start=n == 0, stop=n == len(pairs) - 1)
                        last.then_inc(filled.sem, 1)
                        u = ("P", s, l)
                        pe.wait_ge(*p_ready.at(it, (s, l)))
                        enter(it, u)
                        for b in range(B):
                            last = nc.tensor.transpose(psum(u)[:, 0, b * P:(b + 1) * P], e[:, 0, b, :], ident[:, :])
                        last.then_inc(filled.sem, 1)
                        u = ("X", s, l)
                        took(it, ("P", s, l))
                        enter(it, u)
                        for c in range(C):
                            for b in range(B):
                                last = mm(psum(u)[:, c, b * P:(b + 1) * P], x[s][:, b, c * P:(c + 1) * P], e[:, 1, b, :], start=True, stop=True)
                        last.then_inc(filled.sem, 1)

        @block.scalar
        def _(act):
            activation = nc.scalar.activation
            pro_loads = [0, 0]
            act.wait_ge(par_in, 16 * n_par)
            for j, (name, src, kt, n, scale) in enumerate(jobs):
                pro_loads[j % 2] += 16 * (2 if isinstance(src, tuple) else 1)
                act.wait_ge(w_in[j % 2], pro_loads[j % 2])
                if isinstance(src, tuple):
                    act.wait_ge(w_mm, mm_rank[j] + 1)
                    last = activation(w[name][:, 0], slot[mm_rank[j] % SLOTS][:, :, 0:D], ACT.Copy, scale=scale or 1.0)
                elif isinstance(scale, str):
                    if j == 0:
                        act.wait_ge(w_col, 1)
                    col = ln1_gs if scale == "ln1_gs" else cols[scale][0]
                    for c in range(kt):
                        last = activation(w[name][:, 0, c], staging(j)[:, c], ACT.Copy, scale=col[:, c:c + 1])
                else:
                    last = activation(w[name][:, 0], staging(j), ACT.Copy, scale=scale or 1.0)
                last.then_inc(w_hi, 1)
            act.wait_ge(w_lo, JN)
            act.wait_ge(w_bias, 2)

            with act.Fori(0, steps) as it:

                def hi(u, dst, view=None):
                    act.wait_ge(*filled.at(it, u))
                    activation(dst, psum(u)[:, :, :] if view is None else view, ACT.Copy).then_inc(hi_taken.sem, 1)

                for stage, s, l in stages:
                    if stage == "to_T":
                        u = ("T", s, l)
                        hi(u, xT[s][:, 0])
                        if l == 4:
                            activation(xT_full, psum(u)[:, :, :], ACT.Copy).then_inc(full_taken.sem, 1)
                    elif stage == "qkv":
                        for name, dst in (("q", qT[s][:, 0]), ("k", kT[:, 0].bitcast(F32R))):
                            u = (name, s, l)
                            act.wait_ge(*filled.at(it, u))
                            if name == "k":
                                prev = [k for k in eight if eight.index(k) < eight.index((s, l, 0))]
                                for n in range(2):
                                    mine = [k for k in prev if k[2] % 2 == n]
                                    act.wait_ge(*(kD_in[n].at(it, mine[-1]) if mine else kD_in[n].before(it)))
                            for c in range(C):
                                last = activation(dst[:, c], psum(u)[:, c, :], ACT.Identity, bias=cols[f"b{name}{l}"][0][:, c:c + 1])
                            last.then_inc(hi_taken.sem, 1)
                        hi(("v", s, l), v[s][:, 0].rearrange("p b d -> p (b d)").rearrange("p (c n) -> p c n", c=2))
                    elif stage == "heads":
                        for i in range(B + 1):
                            if i < B:
                                act.wait_ge(*scores_ready.at(it, (s, l, i)))
                                for h in range(H):
                                    last = activation(e[:, i % 2, h, :], e[:, i % 2, h, :], ACT.Exp, bias=neg_max[:, i % 2, h:h + 1],
                                                      accum_out=total[:, i % 2, h:h + 1])
                                last.then_inc(exp_ready.sem, 1)
                            if i >= 1:
                                b = i - 1
                                hi(("P", s, l, b), p16[b % 2][:, 0].rearrange("p (a h) k -> p a (h k)", a=2))
                    elif stage == "mlp":
                        for j in range(NCH):
                            u = ("h", s, l, j)
                            act.wait_ge(*filled.at(it, u))
                            if j >= 2:
                                act.wait_ge(*h_ready.at(it, (s, j - 2)))
                            for i in range(CH):
                                f = j * CH + i
                                last = activation(e[:, j % 2].rearrange("p h k -> p (h k)")[:, i * R:(i + 1) * R], psum(u)[:, i, :],
                                                  ACT.Gelu, bias=cols["b1"][0][:, f:f + 1])
                            last.then_inc(taken[nth[u] % SLOTS].sem, 1)
                            act.wait_ge(*taken[nth[u] % SLOTS].at(it, u))
                            activation(hT[j % 2][:, 0].rearrange("p i r -> p (i r)"), e[:, j % 2].rearrange("p h k -> p (h k)"),
                                       ACT.Copy).then_inc(hi_taken.sem, 1)
                    elif stage == "qk1":
                        u = ("qk", s, l)
                        act.wait_ge(*filled.at(it, u))
                        dst = xn[s][:].rearrange("p (m b) d -> p m (b d)", m=2)
                        if l == 4:
                            last = activation(dst, psum(u)[:, :, :], ACT.Copy)
                        else:
                            activation(dst[:, 0], psum(u)[:, 0, :], ACT.Identity, bias=cols[f"bq{l}"][0][:, 0:1])
                            last = activation(dst[:, 1], psum(u)[:, 1, :], ACT.Identity, bias=cols[f"bk{l}"][0][:, 0:1])
                        last.then_inc(taken[nth[u] % SLOTS].sem, 1)
                    elif stage == "one_head":
                        act.wait_ge(*scores_ready.at(it, (s, l, 0)))
                        for b in range(B):
                            last = activation(e[:, 0, b, :], e[:, 0, b, :], ACT.Exp, bias=neg_max[:, 0, b:b + 1],
                                              accum_out=total[:, 0, b:b + 1])
                        last.then_inc(exp_ready.sem, 1)
                        u = ("P", s, l)
                        act.wait_ge(*filled.at(it, u))
                        activation(e[:, 1, 0:B, :].rearrange("p b k -> p (b k)"), psum(u)[:, 0, :], ACT.Copy).then_inc(taken[nth[u] % SLOTS].sem, 1)
                        hi(("X", s, l), xT[s][:, 0])

        @block.vector
        def _(dve):
            V = nc.vector
            pro = [0]

            def link_pro(ins):
                pro[0] += 1
                ins.then_inc(dve_pro, 1)
                dve.wait_ge(dve_pro, pro[0])

            dve.wait_ge(par_in, 16 * n_par)
            dve.wait_ge(one_made, 5)
            V.tensor_scalar(ln1_gs[:, :], cols["ln1_g"][0][:, :], scale_hd, None, ALU.mult).then_inc(w_col, 1)
            for name in ("bq1", "bq2"):
                link_pro(V.tensor_scalar(cols[name][0][:, :], cols[name][0][:, :], scale_dk, None, ALU.mult))
            link_pro(V.tensor_scalar(cols["bq3"][0][:, :], cols["bq3"][0][:, :], scale_hd, None, ALU.mult))

            def widen(col):
                for c in range(C):
                    last = V.tensor_scalar(bv_wide[:, c, :], ones[:, :], col[:, c:c + 1], None, ALU.mult)
                last.then_inc(w_col, 1)

            for j, (name, src, kt, n, scale) in enumerate(jobs):
                if j in mm_rank:
                    dve.wait_ge(w_mm, mm_rank[j] + 1)
                    ps = slot[mm_rank[j] % SLOTS]
                    if name in ("q0", "k0", "v0", "w1"):
                        col = cols["b1" if name == "w1" else f"b{name}"][0]
                        link_pro(V.tensor_tensor(col[:, :], ps[:, 0, 0:n // P], col[:, :], ALU.add))
                        if name == "q0":
                            link_pro(V.tensor_scalar(col[:, :], col[:, :], scale_hd, None, ALU.mult))
                    if name in ("o0", "o3"):
                        row = rows[f"b{name}"][0]
                        V.tensor_tensor(row[:, :], ps[:, 0, 0:D], row[:, :], ALU.add).then_inc(w_bias, 1)
                dve.wait_ge(w_hi, j + 1)
                high = w[name][:, 0].bitcast(F32)
                if isinstance(src, tuple):
                    last = V.scalar_tensor_tensor(out=w[name][:, 1], in0=slot[mm_rank[j] % SLOTS][:, :, 0:D], scalar=scale or 1.0,
                                                  in1=high, op0=ALU.mult, op1=ALU.subtract)
                elif isinstance(scale, str):
                    col = ln1_gs if scale == "ln1_gs" else cols[scale][0]
                    for c in range(kt):
                        last = V.scalar_tensor_tensor(out=w[name][:, 1, c], in0=staging(j)[:, c], scalar=col[:, c:c + 1],
                                                      in1=high[:, c], op0=ALU.mult, op1=ALU.subtract)
                else:
                    last = V.scalar_tensor_tensor(out=w[name][:, 1], in0=staging(j), scalar=scale or 1.0, in1=high,
                                                  op0=ALU.mult, op1=ALU.subtract)
                last.then_inc(w_lo, 1)
                if name in ("v0", "v3"):
                    if name == "v3":
                        dve.wait_ge(w_bias, 1)
                    widen(cols[f"b{name}"][0])

            with dve.Fori(0, steps) as it:
                chain = Chain(dve, dve_step, it, DVE_LINKS * STREAMS)
                link = chain.link

                def done(instruction, signal, key):
                    instruction.then_inc(signal.sem, 1)
                    dve.wait_ge(*signal.at(it, key))

                def took(instruction, u):
                    done(instruction, taken[nth[u] % SLOTS], u)

                def lo(u, dst, high, view=None):
                    dve.wait_ge(*hi_taken.at(it, u))
                    if u[0] == "T" and u[2] == 4:
                        dve.wait_ge(*full_taken.at(it, u))
                    took(V.tensor_tensor(dst, psum(u)[:, :, :] if view is None else view, high, ALU.subtract), u)

                def statistics(s, key):
                    for b in range(B):
                        last = V.bn_stats(stats[:, b, :], x[s][:, b, :])
                    link(last)
                    even_mean, even_m2, odd_mean, odd_m2 = (stats[:, :, n] for n in (1, 2, 4, 5))
                    V.tensor_tensor(mean[:, :], even_mean, odd_mean, ALU.add)
                    V.tensor_tensor(gap[:, :], even_mean, odd_mean, ALU.subtract)
                    link(V.tensor_tensor(var[:, :], even_m2, odd_m2, ALU.add))
                    V.tensor_scalar(mean[:, :], mean[:, :], 0.5, None, ALU.mult)
                    V.scalar_tensor_tensor(out=gap[:, :], in0=gap[:, :], scalar=0.25, in1=gap[:, :], op0=ALU.mult, op1=ALU.mult)
                    link(V.tensor_scalar(var[:, :], var[:, :], 1.0 / D, EPS, ALU.mult, ALU.add))
                    done(V.tensor_tensor(var[:, :], var[:, :], gap[:, :], ALU.add), var_ready, (s, key))
                    dve.wait_ge(*rstd_ready.at(it, (s, key)))

                def masked(s, kind, it):
                    if kind == "L0":
                        link(V.tensor_scalar(bias[s][:, :, :], adj[s][:, :, :], 0.1, None, ALU.mult))
                        link(V.tensor_tensor(bias[s][:, :, :], bias[s][:, :, :], adj[s][:, :, :], ALU.mult))
                        link(V.tensor_scalar(xn[s][:, 0:2].rearrange("p a d -> p (a d)"), adj[s][:].rearrange("p b k -> p (b k)"), 0.0, None, ALU.is_gt))
                        m = xn[s][:, 0:2].rearrange("p a d -> p (a d)")
                        bf = bias[s][:].rearrange("p b k -> p (b k)")
                        link(V.tensor_tensor(bf, bf, m, ALU.mult))
                        link(V.tensor_scalar(m, m, 1.0, -MASKED, ALU.subtract, ALU.mult))
                        link(V.tensor_tensor(bf, bf, m, ALU.add))
                    else:
                        link(V.tensor_scalar(bias[s][:, :, :], adj[s][:, :, :], 0.0, MASKED, ALU.is_equal, ALU.mult))

                for stage, s, l in stages:
                    if stage == "load":
                        dve.wait_ge(*x_in.at(it, (s, l)))
                        dve.wait_ge(*adj_in.at(it, (s, l)))
                        dve.wait_ge(*filled.before(it))
                        masked(s, "L0", it)
                    elif stage in ("norm_in", "norm_mid"):
                        key = norm_key[stage, l]
                        statistics(s, key)
                        for b in range(B):
                            last = V.tensor_scalar(xn[s][:, b, :], x[s][:, b, :], mean[:, b:b + 1], rstd[:, b:b + 1], ALU.subtract, ALU.mult)
                        done(last, rows_ready, (s, key))
                    elif stage == "norm_out":
                        statistics(s, l)
                        g, b_ = rows[f"g{l}"][0], rows[f"b_{l}"][0]
                        for b in range(B):
                            last = V.scalar_tensor_tensor(out=x[s][:, b, :], in0=x[s][:, b, :], scalar=mean[:, b:b + 1], in1=g[:, :],
                                                          op0=ALU.subtract, op1=ALU.mult)
                        link(last)
                        for b in range(B):
                            last = V.scalar_tensor_tensor(out=x[s][:, b, :], in0=x[s][:, b, :], scalar=rstd[:, b:b + 1], in1=b_[:, :],
                                                          op0=ALU.mult, op1=ALU.add)
                        done(last, rows_ready, (s, l))
                    elif stage == "to_T":
                        if l == 1:
                            masked(s, "L1", it)
                        lo(("T", s, l), xT[s][:, 1], xT[s][:, 0].bitcast(F32))
                    elif stage == "qkv":
                        for name, dst, high in (("q", qT[s][:, 1], qT[s][:, 0].bitcast(F32)),
                                                ("k", kT[:, 1].bitcast(F32R), kT[:, 0])):
                            u = (name, s, l)
                            dve.wait_ge(*hi_taken.at(it, u))
                            for c in range(C):
                                last = V.scalar_tensor_tensor(out=dst[:, c], in0=psum(u)[:, c, :], scalar=cols[f"b{name}{l}"][0][:, c:c + 1],
                                                              in1=high[:, c], op0=ALU.add, op1=ALU.subtract)
                            took(last, u)
                        u = ("v", s, l)
                        dve.wait_ge(*hi_taken.at(it, u))
                        flat = [v[s][:, p].rearrange("p (a b) d -> p a (b d)", a=2) for p in range(3)]
                        rest = xn[s][:].rearrange("p (a b) d -> p a (b d)", a=2)
                        took(V.tensor_tensor(rest, psum(u)[:, :, :], flat[0], ALU.subtract), u)
                        link(V.tensor_copy(flat[1], rest))
                        done(V.tensor_tensor(flat[2], rest, flat[1], ALU.subtract), v_ready, (s, l))
                    elif stage == "heads":
                        for i in range(B + 2):
                            if i < B:
                                n = i % 2
                                u = ("S", s, l, i)
                                dve.wait_ge(*filled.at(it, u))
                                took(V.tensor_tensor(e[:, n], heads(psum(u)[:, :, :].rearrange("p a n -> p (a n)")),
                                                     bias[s][:, i, :].unsqueeze(1).broadcast_to([P, H, P]), ALU.add), u)
                                done(V.tensor_reduce(out=neg_max[:, n, :], in_=e[:, n], op=ALU.max, axis=AX.X, negate=True),
                                     scores_ready, (s, l, i))
                            if 1 <= i <= B:
                                b = i - 1
                                u = ("P", s, l, b)
                                lo(u, p16[b % 2][:, 1].rearrange("p (a h) k -> p a (h k)", a=2),
                                   p16[b % 2][:, 0].rearrange("p (a h) k -> p a (h k)", a=2))
                                link(V.reciprocal(rinv[:, b % 2, :], total[:, b % 2, :]))
                            if i >= 2:
                                b = i - 2
                                u = ("O", s, l, b)
                                dve.wait_ge(*filled.at(it, u))
                                took(V.tensor_tensor(xn[s][:, b, :].rearrange("p (h d) -> p h d", d=HD),
                                                     psum(u)[:, 0, 0:D].rearrange("p (h d) -> p h d", d=HD),
                                                     rinv[:, b % 2, :].unsqueeze(2).broadcast_to([P, H, HD]), ALU.mult), u)
                    elif stage == "out_proj":
                        u = ("o", s, l)
                        if l in (0, 3, 4):
                            dve.wait_ge(*b_added.at(it, (s, l)))
                        dve.wait_ge(*filled.at(it, u))
                        rows_x = x[s][:].rearrange("p (a b) d -> p a (b d)", a=2)
                        took(V.tensor_tensor(rows_x, psum(u)[:, :, :], rows_x, ALU.add), u)
                    elif stage == "mlp":
                        for j in range(NCH):
                            u = ("h", s, l, j)
                            dve.wait_ge(*hi_taken.at(it, u))
                            done(V.tensor_tensor(hT[j % 2][:, 1].rearrange("p i r -> p (i r)"), e[:, j % 2].rearrange("p h k -> p (h k)"),
                                                 hT[j % 2][:, 0].bitcast(F32).rearrange("p i r -> p (i r)"), ALU.subtract), h_ready, (s, j))
                        u = ("y", s, l)
                        dve.wait_ge(*b_added.at(it, (s, "mid")))
                        dve.wait_ge(*y_done.at(it, (s, l)))
                        rows_x = x[s][:].rearrange("p (a b) d -> p a (b d)", a=2)
                        took(V.tensor_tensor(rows_x, psum(u)[:, :, :], rows_x, ALU.add), u)
                    elif stage == "one_head":
                        u = ("S", s, l)
                        dve.wait_ge(*filled.at(it, u))
                        took(V.tensor_tensor(e[:, 0, 0:B, :], heads(psum(u)[:, 0, :]), bias[s][:, :, :], ALU.add), u)
                        done(V.tensor_reduce(out=neg_max[:, 0, 0:B], in_=e[:, 0, 0:B, :], op=ALU.max, axis=AX.X, negate=True),
                             scores_ready, (s, l, 0))
                        dve.wait_ge(*exp_ready.at(it, (s, l, 0)))
                        link(V.reciprocal(rinv[:, 0, 0:B], total[:, 0, 0:B]))
                        p = e[:, 0, 0:B, :]
                        r = rinv[:, 0, 0:B].unsqueeze(2).broadcast_to([P, B, P])
                        if l == 4:
                            done(V.tensor_tensor(p, p, r, ALU.mult), p_ready, (s, l))
                        else:
                            link(V.tensor_tensor(p, p, r, ALU.mult))
                            link(V.tensor_scalar(e[:, 1, 0:B, :], adj[s][:, :, :], 0.0, None, ALU.not_equal))
                            done(V.tensor_tensor(p, p, e[:, 1, 0:B, :], ALU.mult), p_ready, (s, l))
                        lo(("X", s, l), xT[s][:, 1], xT[s][:, 0].bitcast(F32))
                chain.end()


DVE_LINKS = 46

LAYERED = {"L1_gnn_Wq": True, "L1_gnn_Wk": True, "L1_gnn_Wc": True, "L1_gnn_bq": False, "L1_gnn_bk": False,
           "L1_gnn_ln_g": False, "L1_gnn_ln_b": False}
COLUMNS = ("L0_gnn_ln1_g", "L0_gnn_ln1_b", "L0_gnn_ln2_g", "L0_gnn_ln2_b", "L0_gnn_bq", "L0_gnn_bk", "L0_gnn_bv", "L0_gnn_b1",
           "L1_gnn_bq0", "L1_gnn_bk0", "L1_gnn_bq1", "L1_gnn_bk1", "L2_gnn_bq", "L2_gnn_bk", "L2_gnn_bv")
TRANSPOSED = ("L3_gnn_Wq", "L3_gnn_Wk", "L3_gnn_Wv")


def laid_out(inputs):
    arrays = {}
    for name, a in inputs.items():
        a = np.asarray(a)
        if name in LAYERED:
            for n in range(a.shape[0]):
                arrays[f"{name}{'T' if LAYERED[name] else ''}{n}"] = np.ascontiguousarray(a[n].T)
        elif name in TRANSPOSED:
            arrays[f"{name}T"] = np.ascontiguousarray(a.T)
        else:
            arrays[name] = np.ascontiguousarray(a)
    for name in COLUMNS:
        arrays[name + "_col"] = np.ascontiguousarray(arrays.pop(name).reshape(-1, P).T)
    return arrays


def kernel(**inputs):
    import concourse.bacc as bacc
    from concourse.bass_utils import run_bass_kernel_spmd

    nc = bacc.Bacc("TRN2", target_bir_lowering=False, num_devices=1)
    arrays = laid_out(inputs)
    t = {n: nc.dram_tensor(f"in_{n}", a.shape, mybir.dt.from_np(a.dtype), kind="ExternalInput").ap() for n, a in arrays.items()}
    graphs = arrays["x"].shape[0]
    out = nc.dram_tensor("out", (graphs, P, D), F32, kind="ExternalOutput").ap()
    mk_kernel(nc, graphs // (B * STREAMS), t, out)
    r = run_bass_kernel_spmd(nc, [{f"in_{n}": a for n, a in arrays.items()}], core_ids=[0])
    return r.results[0]["out"]
```

```python
from contextlib import ExitStack

import numpy as np

import concourse.bass as bass
from concourse import mybir

F32 = mybir.dt.float32
F32R = mybir.dt.float32r
F16 = mybir.dt.float16
BF16 = mybir.dt.bfloat16
I32 = mybir.dt.int32
ALU = mybir.AluOpType
ACT = mybir.ActivationFunctionType
AX = mybir.AxisListType

P = 128
D = 256
C = D // P
B = 4
R = B * P
H = 8
HD = D // H
HC = P // HD
FF = 4 * D
FT = FF // P
DK = 128
EPS = 1e-5
MASKED = -1e30
STREAMS = 2
SLOTS = 3


COST = {"load": 2.0, "norm_stat": 1.5, "norm_apply": 1.5, "to_T": 1.5, "q": 2.6, "k": 2.6, "v": 2.6, "heads": 3.0, "out_proj": 2.6,
        "mlp": 2.6, "qk1": 2.6, "S1": 1.5, "P1": 1.5, "X1": 1.7, "store": 0.5}
LINKS = {"load": 6, "norm_stat": 3, "norm_out": 1, "mask": 1, "v": 1, "heads": 1, "P1": 1, "P1_masked": 2}


def first_layer(s):
    return (
        [("load", s, 0, 0), ("norm_stat", s, 0, 0), ("norm_apply", s, 0, 0), ("to_T", s, "0", 0), ("k", s, 0, 0), ("q", s, 0, 0), ("v", s, 0, 0)]
        + [("heads", s, 0, i) for i in range(B + 2)]
        + [("to_T", s, "0a", 0), ("out_proj", s, 0, 0), ("norm_stat", s, "mid", 0), ("norm_apply", s, "mid", 0), ("to_T", s, "0m", 0)]
        + [("mlp", s, 0, i) for i in range(FT + 2)]
    )


def later_layers(s):
    def one_head(l):
        return [(n, s, l, 0) for n in ("to_T", "qk1", "S1", "P1", "X1", "out_proj", "norm_stat", "norm_apply")]

    return (
        one_head(1) + one_head(2)
        + [(n, s, 3, 0) for n in ("to_T", "k", "q", "v")] + [("heads", s, 3, i) for i in range(B + 2)]
        + [("to_T", s, "3a", 0), ("out_proj", s, 3, 0), ("norm_stat", s, 3, 0), ("norm_apply", s, 3, 0)]
        + one_head(4) + [("store", s, 4, 0)]
    )


def pair(a, b):
    front, back = first_layer(a), later_layers(b)
    n, m = front.index(("heads", a, 0, B + 1)) + 1, back.index(("k", b, 3, 0))
    return mixed(front[:n], back[:m]) + mixed(front[n:], back[m:])


def mixed(a, b):
    out, done = [], [0.0, 0.0]
    total = [max(sum(COST[x[0]] for x in part), 1.0) for part in (a, b)]
    at = [0, 0]
    while at[0] < len(a) or at[1] < len(b):
        n = 0 if at[1] == len(b) or (at[0] < len(a) and done[0] / total[0] < done[1] / total[1]) else 1
        stage = (a, b)[n][at[n]]
        out.append(stage)
        done[n] += COST[stage[0]]
        at[n] += 1
    return out


class Body:

    def __init__(self, stages, before):
        self.stages, self.before = stages, before
        self.it, self.now = 0, 0

    def walk(self, it=0):
        self.it = it
        for self.now, stage in enumerate(self.stages):
            yield stage


class Signal:

    START = 1

    def __init__(self, sem, keys, bodies, unit=1):
        self.sem, self.unit = sem, unit
        self.rank, self.stage, self.size = {}, {}, {}
        for body in bodies:
            found = list(keys(body.stages))
            self.rank[body] = {key: n for n, (_, key) in enumerate(found)}
            self.stage[body] = {key: stage for stage, key in found}
            self.size[body] = len(found) * unit
            assert len(self.rank[body]) == len(found)

    def before(self, body):
        base = sum(self.size[b] * times for b, times in body.before) + self.START
        return self.sem, body.it * self.size[body] + base

    def so_far(self, body):
        sem, base = self.before(body)
        return sem, base + sum(stage < body.now for stage in self.stage[body].values()) * self.unit

    def at(self, body, key):
        sem, base = self.before(body)
        if self.stage[body].get(key, len(body.stages)) > body.now:
            return sem, base
        return sem, base + (self.rank[body][key] + 1) * self.unit


class Chain:

    def __init__(self, engine, signal):
        self.engine, self.steps = engine, signal

    def start(self, body):
        self.body, self.n = body, 0

    def link(self, instruction):
        sem, base = self.steps.before(self.body)
        instruction.then_inc(sem, 1)
        self.n += 1
        self.engine.wait_ge(sem, base + self.n)

    def end(self):
        assert self.n == self.steps.size[self.body], (self.n, self.steps.size[self.body])


def links_of(stage):
    name, s, l, i = stage
    n = LINKS.get(name, 0)
    if name == "norm_apply":
        n = LINKS["norm_out"] if l in (1, 2, 3, 4) else 0
    if name == "to_T":
        n = LINKS["mask"] if l == 1 else 0
    if name == "heads":
        n = LINKS["heads"] if 1 <= i <= B else 0
    if name == "P1":
        n = LINKS["P1"] if l == 4 else LINKS["P1"] + LINKS["P1_masked"]
    return n


def units_of(stage):
    name, s, l, i = stage
    if name == "heads":
        return [("S", s, l, i)] * (i < B) + [("O", s, l, i - 2)] * (i >= 2) + [("P", s, l, i - 1)] * (1 <= i <= B)
    if name == "mlp":
        return [("h", s, l, i)] * (i < FT)
    return {"to_T": [("T", s, l)], "q": [("q", s, l)], "k": [("k", s, l)], "v": [("v", s, l)], "out_proj": [("o", s, l)],
            "qk1": [("qk", s, l)], "S1": [("S", s, l)], "P1": [("P", s, l)], "X1": [("X", s, l)]}.get(name, [])


def mk_kernel(nc, steps, t, out):
    scale_hd = float(1.0 / np.sqrt(HD))
    scale_dk = float(1.0 / np.sqrt(DK))
    scale_d = float(1.0 / np.sqrt(D))
    ctx = ExitStack()
    with ctx:
        def sb(name, shape, dt):
            return ctx.enter_context(nc.sbuf_tensor(name, shape, dt))

        def sem(name):
            return ctx.enter_context(nc.semaphore(name))

        jobs = [
            ("q0", "L0_gnn_wq", C, D, "ln1_gs"), ("k0", "L0_gnn_wk", C, D, "ln1_g"), ("v0", "L0_gnn_wv", C, D, "ln1_g"),
            ("o0", "L0_gnn_wo", C, D, None), ("w1", "L0_gnn_w1", C, FF, "ln2_g"), ("w2", "L0_gnn_w2", FT, D, None),
            ("q1", "L1_gnn_WqT0", C, DK, scale_dk), ("k1", "L1_gnn_WkT0", C, DK, None), ("o1", "L1_gnn_WcT0", C, D, None),
            ("q2", "L1_gnn_WqT1", C, DK, scale_dk), ("k2", "L1_gnn_WkT1", C, DK, None), ("o2", "L1_gnn_WcT1", C, D, None),
            ("q3", "L2_gnn_Wq", C, D, scale_hd), ("k3", "L2_gnn_Wk", C, D, None), ("v3", "L2_gnn_Wv", C, D, None),
            ("o3", "L2_gnn_Wo", C, D, None),
            ("q4", ("L3_gnn_WqT", "L3_gnn_WkT"), C, D, scale_d), ("o4", ("L3_gnn_WvT", "L3_gnn_Wo"), C, D, None),
        ]
        w = {j[0]: sb(f"w_{j[0]}", [P, 2, j[2], j[3]], F32R) for j in jobs}

        cols = {}
        for name, src, n in (
            ("ln1_g", "L0_gnn_ln1_g", C), ("ln1_b", "L0_gnn_ln1_b", C), ("ln2_g", "L0_gnn_ln2_g", C),
            ("ln2_b", "L0_gnn_ln2_b", C), ("bq0", "L0_gnn_bq", C), ("bk0", "L0_gnn_bk", C), ("bv0", "L0_gnn_bv", C),
            ("b1", "L0_gnn_b1", FT), ("bq1", "L1_gnn_bq0", 1), ("bk1", "L1_gnn_bk0", 1), ("bq2", "L1_gnn_bq1", 1),
            ("bk2", "L1_gnn_bk1", 1), ("bq3", "L2_gnn_bq", C), ("bk3", "L2_gnn_bk", C), ("bv3", "L2_gnn_bv", C),
        ):
            cols[name] = (sb(f"c_{name}", [P, n], F32), src)
        ln1_gs = sb("ln1_gs", [P, C], F32)
        rows = {}
        for name, src in (
            ("bo0", "L0_gnn_bo"), ("b2", "L0_gnn_b2"), ("bo3", "L2_gnn_bo"), ("bo4", "L3_gnn_bo"),
            ("g1", "L1_gnn_ln_g0"), ("b_1", "L1_gnn_ln_b0"), ("g2", "L1_gnn_ln_g1"), ("b_2", "L1_gnn_ln_b1"),
            ("g3", "L2_gnn_gamma"), ("b_3", "L2_gnn_beta"), ("g4", "L3_gnn_gamma"), ("b_4", "L3_gnn_beta"),
        ):
            rows[name] = (sb(f"r_{name}", [P, D], F32), src)
        ident = sb("ident", [P, P], F32)
        started = sb("started", [P, 32], mybir.dt.uint8)
        minus_half = sb("minus_half", [P, B], F32)

        x = [sb(f"x{s}", [P, B, D], F32) for s in range(STREAMS)]
        xn = [sb(f"xn{s}", [P, B, D], F32) for s in range(STREAMS)]
        xT = [sb(f"xT{s}", [P, 2, C, R], F32R) for s in range(STREAMS)]
        adj = [sb(f"adj{s}", [P, B, P], I32) for s in range(STREAMS)]
        bias = [sb(f"bias{s}", [P, B, P], F32) for s in range(STREAMS)]
        qT = sb("qT", [P, 2, C, R], F32R)
        v = sb("v", [P, 3, B, D], BF16)
        kT = sb("kT", [P, 2, C, R], F32)
        kD = [sb(f"kD{n}", [P, 2, C, HC, P], F32R) for n in range(2)]
        e = sb("e", [P, 2, H, P], F32)
        e1 = sb("e1", [P, 2, B, P], F32)
        p16 = sb("p16", [P, 2, H, P], F16)
        h32 = sb("h32", [P, 2, R], F32)
        hT = [sb(f"hT{n}", [P, 2, R], F32R) for n in range(2)]
        bv_wide = xn[0][:, 0, :].rearrange("p (c k) -> p c k", c=C)
        stats = [sb(f"stats{s}", [P, B, 6], F32) for s in range(STREAMS)]
        mean = [sb(f"mean{s}", [P, B], F32) for s in range(STREAMS)]
        gap = [sb(f"gap{s}", [P, B], F32) for s in range(STREAMS)]
        var = [sb(f"var{s}", [P, B], F32) for s in range(STREAMS)]
        rstd = [sb(f"rstd{s}", [P, B], F32) for s in range(STREAMS)]
        neg_max = sb("neg_max", [P, 3, H], F32)
        total = sb("total", [P, 3, H], F32)
        rinv = sb("rinv", [P, 3, H], F32)
        xT_full = kT[:, 0]

        slot = [ctx.enter_context(nc.psum_tensor(f"slot{n}", [P, 2, 512], F32)) for n in range(SLOTS + 1)]

        whole = pair(0, 1) + pair(1, 0)
        first = Body(first_layer(0) + pair(1, 0), [])
        loop = Body(whole, [(first, 1)])
        last_ = Body(later_layers(1), [(first, 1), (loop, steps - 1)])
        bodies = [first, loop, last_]
        nth = {u: n for n, u in enumerate(u for st in whole for u in units_of(st))}
        in_slot = {}
        for body in bodies:
            held = {}
            for st in body.stages:
                for u in units_of(st):
                    in_slot[body, u] = held.get(nth[u] % SLOTS)
                    held[nth[u] % SLOTS] = u

        def slot_of(u):
            return SLOTS if u[0] == "y" else nth[u] % SLOTS

        def psum(u):
            return slot[slot_of(u)]

        def signal(name, key_of, unit=1):
            return Signal(sem(name), lambda stages: [(n, k) for n, st in enumerate(stages) for k in key_of(st)], bodies, unit)

        def when(*names, **at):
            return lambda st: [(st[1], st[2])] if st[0] in names and ("l" not in at or st[2] in at["l"]) else []

        def b_after(body_st):
            name, s, l, i = body_st
            return [(s, l)] if (name == "norm_apply" and l in (0, "mid")) or (name == "k" and l == 3) or (name == "X1" and l == 4) else []

        filled = signal("filled", units_of)
        taken = [signal(f"taken{n}", lambda st, n=n: [u for u in units_of(st) if nth[u] % SLOTS == n]) for n in range(SLOTS)]
        taken.append(signal("y_taken", lambda st: [("y", st[1], 0)] if st[0] == "mlp" and st[3] == FT + 1 else []))
        hi_taken = signal("hi_taken", lambda st: [u for u in units_of(st) if u[0] in ("T", "q", "k", "v", "h", "X") or (u[0] == "P" and len(u) == 4)])
        full_taken = signal("full_taken", when("to_T", l=(4,)))
        y_done = signal("y_done", lambda st: [(st[1], st[2])] if st[0] == "mlp" and st[3] == FT + 1 else [])
        x_in = signal("x_in", when("load"), 16)
        adj_in = signal("adj_in", when("load"), 16)
        stored = signal("stored", when("store"), 16)
        kD_in = [signal(f"kD_in{n}", lambda st, n=n: [(st[1], st[2], st[3])] if st[0] == "heads" and st[3] < B and st[3] % 2 == n else [], 16 * HC)
                 for n in range(2)]
        var_ready = signal("var_ready", when("norm_stat"))
        rstd_ready = signal("rstd_ready", when("norm_stat"))
        rows_ready = signal("rows_ready", when("norm_apply"))
        b_added = signal("b_added", b_after)
        eight = lambda st: [(st[1], st[2], st[3])] if st[0] == "heads" and st[3] < B else []
        scores_ready = signal("scores_ready", lambda st: eight(st) + when("S1")(st))
        exp_ready = signal("exp_ready", lambda st: eight(st) + when("S1")(st))
        p_ready = signal("p_ready", when("P1"))
        v_ready = signal("v_ready", when("v"))
        h_ready = signal("h_ready", lambda st: [(st[1], st[3])] if st[0] == "mlp" and st[3] < FT else [])
        dve_step = signal("dve_step", lambda st: [(st, n) for n in range(links_of(st))])
        pool_pro = sem("pool_pro")
        signals = [dve_step, filled, *taken, hi_taken, full_taken, y_done, x_in, adj_in, stored, *kD_in, var_ready, rstd_ready, rows_ready,
                   b_added, scores_ready, exp_ready, p_ready, v_ready, h_ready]
        par_in, one_made = sem("par_in"), sem("const_made")
        w_in = [sem(f"w_in{n}") for n in range(2)]
        w_mm, w_hi, w_lo, w_col, w_bias = sem("w_mm"), sem("w_hi"), sem("w_lo"), sem("w_col"), sem("w_bias")
        dve_pro = sem("dve_pro")
        n_par = len(cols) + len(rows)
        JN = len(jobs)

        def staging(j):
            base = kT[:].rearrange("p a c r -> p (a c r)") if j % 2 == 0 else e[:].rearrange("p a h k -> p (a h k)")
            _, _, kt, n, _ = jobs[j]
            return base[:, 0:kt * n].rearrange("p (k n) -> p k n", k=kt)

        def staging2(j):
            base = kT[:].rearrange("p a c r -> p (a c r)") if j % 2 == 0 else e[:].rearrange("p a h k -> p (a h k)")
            return base[:, C * D:2 * C * D].rearrange("p (k n) -> p k n", k=C)

        MM_JOBS = [j for j, jb in enumerate(jobs) if jb[0] in ("q0", "k0", "v0", "o0", "w1", "o3", "q4", "o4")]
        mm_rank = {j: n for n, j in enumerate(MM_JOBS)}

        block = ctx.enter_context(nc.Block())

        @block.sync
        def _(sp):
            for name, (dst, src) in cols.items():
                sp.dma_start(dst[:, :], t[src + "_col"]).then_inc(par_in, 16)
            for name, (dst, src) in rows.items():
                sp.dma_start(dst[:, :], t[src].unsqueeze(0).broadcast_to([P, D])).then_inc(par_in, 16)
            for j, (name, src, kt, n, _) in enumerate(jobs):
                if j >= 2:
                    sp.wait_ge(w_lo, j - 1)
                    sp.wait_ge(w_hi, j - 1)
                if isinstance(src, tuple):
                    sp.dma_start(staging(j), t[src[0]].rearrange("(k p) n -> p k n", p=P)).then_inc(w_in[j % 2], 16)
                    sp.dma_start(staging2(j), t[src[1]].rearrange("(k p) n -> p k n", p=P)).then_inc(w_in[j % 2], 16)
                else:
                    sp.dma_start(staging(j), t[src].rearrange("(k p) n -> p k n", p=P)).then_inc(w_in[j % 2], 16)
            x_v = t["x"].rearrange("(i b) n f -> i n b f", b=B)
            adj_v = t["adj"].rearrange("(i b) n m -> i n b m", b=B)
            out_v = out.rearrange("(i b) n f -> i n b f", b=B)
            sp.wait_ge(w_lo, JN)

            def run(body, it):
                def group(s, tail):
                    if body is first:
                        return s
                    if body is last_:
                        return (steps - 1) * STREAMS + s
                    return it * STREAMS + s + (0 if tail and s == 1 else STREAMS)

                def keys_to_blocks(s, l, b):
                    for h in range(HC):
                        q = slice(h * HD, (h + 1) * HD)
                        sp.dma_start(
                            kD[b % 2][q, :, :, h, :].bitcast(F32).rearrange("p a c k -> p (a c) k"),
                            kT[q, :, :, b * P:(b + 1) * P].rearrange("p a c k -> p (a c) k"),
                        ).then_inc(kD_in[b % 2].sem, 16)

                for stage, s, l, i in body.walk(it):
                    if stage == "load":
                        sp.wait_ge(*stored.so_far(body))
                        sp.dma_start(x[s][:, :, :], x_v[group(s, False)]).then_inc(x_in.sem, 16)
                        sp.dma_start(adj[s][:, :, :], adj_v[group(s, False)]).then_inc(adj_in.sem, 16)
                    elif stage == "k":
                        sp.wait_ge(*taken[slot_of(("k", s, l))].at(body, ("k", s, l)))
                        for b in range(2):
                            keys_to_blocks(s, l, b)
                    elif stage == "heads" and i + 2 < B:
                        sp.wait_ge(*filled.at(body, ("S", s, l, i)))
                        keys_to_blocks(s, l, i + 2)
                    elif stage == "store":
                        sp.wait_ge(*rows_ready.at(body, (s, 4)))
                        sp.dma_start(out_v[group(s, True)], x[s][:, :, :]).then_inc(stored.sem, 16)

            run(first, 0)
            with sp.Fori(0, steps - 1) as it:
                run(loop, it)
            run(last_, 0)
            last_.now = len(last_.stages)
            sp.wait_ge(*stored.so_far(last_))

        @block.gpsimd
        def _(pool):
            nc.gpsimd.memset(ident[:, :], 0.0).then_inc(pool_pro, 1)
            pool.wait_ge(pool_pro, 1)
            nc.gpsimd.affine_select(out=ident[:, :], in_=ident[:, :], compare_op=ALU.not_equal, fill=1.0, base=0,
                                    pattern=[[-1, P]], channel_multiplier=1).then_inc(one_made, 1)
            nc.gpsimd.memset(minus_half[:, :], -0.5).then_inc(one_made, 1)
            for n in range(2):
                nc.gpsimd.memset(kD[n][:].bitcast(F32), 0.0).then_inc(one_made, 1)
            for n, signal in enumerate(signals):
                nc.gpsimd.memset(started[:, n:n + 1], 0).then_inc(signal.sem, Signal.START)
            pool.wait_ge(one_made, 4)
            pool.wait_ge(par_in, 16 * n_par)
            pool.wait_ge(w_bias, 2)

            def add_rows(s, row):
                nc.gpsimd.tensor_tensor(x[s][:, :, :], x[s][:, :, :],
                                        rows[row][0][:, :].unsqueeze(1).broadcast_to([P, B, D]), ALU.add).then_inc(b_added.sem, 1)

            def run(body, it):
                for stage, s, l, i in body.walk(it):
                    if stage == "norm_stat":
                        pool.wait_ge(*var_ready.at(body, (s, l)))
                        nc.gpsimd.tensor_tensor(rstd[s][:, :], var[s][:, :], minus_half[:, :], ALU.pow).then_inc(rstd_ready.sem, 1)
                    elif stage == "norm_apply" and l in (0, "mid"):
                        pool.wait_ge(*rows_ready.at(body, (s, l)))
                        add_rows(s, "bo0" if l == 0 else "b2")
                    elif stage == "k" and l == 3:
                        pool.wait_ge(*filled.at(body, ("T", s, 3)))
                        add_rows(s, "bo3")
                    elif stage == "X1" and l == 4:
                        pool.wait_ge(*filled.at(body, ("X", s, 4)))
                        add_rows(s, "bo4")

            run(first, 0)
            with pool.Fori(0, steps - 1) as it:
                run(loop, it)
            run(last_, 0)

        @block.tensor
        def _(pe):
            mm = nc.tensor.matmul

            def three(dst, a, b_, first, last, **kw):
                mm(dst, a(1), b_(0), start=first, stop=False, **kw)
                mm(dst, a(0), b_(1), start=False, stop=False, **kw)
                return mm(dst, a(0), b_(0), start=False, stop=last, **kw)

            pe.wait_ge(one_made, 4)
            pe.wait_ge(par_in, 16 * n_par)
            w_loads = [0, 0]
            for j, (name, src, kt, n, _) in enumerate(jobs):
                w_loads[j % 2] += 16 * (2 if isinstance(src, tuple) else 1)
                if j not in mm_rank:
                    continue
                pe.wait_ge(w_in[j % 2], w_loads[j % 2])
                if mm_rank[j] >= SLOTS:
                    pe.wait_ge(w_lo, MM_JOBS[mm_rank[j] - SLOTS] + 1)
                    pe.wait_ge(w_hi, MM_JOBS[mm_rank[j] - SLOTS] + 1)
                ps = slot[mm_rank[j] % SLOTS]
                st = staging(j)
                if name in ("q0", "k0", "v0", "w1"):
                    b_col = cols["ln2_b" if name == "w1" else "ln1_b"][0]
                    for m in range(n // P):
                        for c in range(C):
                            last = mm(ps[:, 0, m:m + 1], st[:, c, m * P:(m + 1) * P], b_col[:, c:c + 1],
                                      start=c == 0, stop=c == C - 1)
                elif name in ("o0", "o3"):
                    pe.wait_ge(w_col, 2 if name == "o0" else 3)
                    for c in range(C):
                        last = mm(ps[:, 0, 0:D], bv_wide[:, c, :], st[:, c, :], start=c == 0, stop=c == C - 1)
                else:
                    st2 = staging2(j)
                    for m in range(C):
                        for c in range(C):
                            last = mm(ps[:, m, 0:D], st[:, c, m * P:(m + 1) * P], st2[:, c, :], start=c == 0, stop=c == C - 1)
                last.then_inc(w_mm, 1)
            pe.wait_ge(w_lo, JN)

            def run(body, it):
                def enter(u):
                    if u[0] == "y":
                        pe.wait_ge(*taken[SLOTS].so_far(body))
                    elif in_slot[body, u] is None:
                        pe.wait_ge(*taken[slot_of(u)].before(body))
                    else:
                        pe.wait_ge(*taken[slot_of(u)].at(body, in_slot[body, u]))

                def took(u):
                    pe.wait_ge(*taken[slot_of(u)].at(body, u))

                def half(u, n):
                    return psum(u)[:, n, :]

                def rows_out(u, X, W):
                    for b in range(B):
                        for c in range(C):
                            last = three(psum(u)[:, b // 2, b % 2 * D:(b % 2 + 1) * D], lambda p: X[:, p, c, b * P:(b + 1) * P],
                                         lambda p: W[:, p, c, :], c == 0, c == C - 1)
                    return last

                for stage, s, l, i in body.walk(it):
                    X = xT[s]
                    if stage == "to_T":
                        u = ("T", s, l)
                        src = x[s]
                        if l in ("0", "0m"):
                            pe.wait_ge(*rows_ready.at(body, (s, 0 if l == "0" else "mid")))
                            src = xn[s]
                        elif l in ("0a", "3a"):
                            took(("O", s, int(l[0]), B - 1))
                            src = xn[s]
                        elif l == 1:
                            took(("y", s, 0))
                        else:
                            pe.wait_ge(*rows_ready.at(body, (s, l - 1)))
                        enter(u)
                        for c in range(C):
                            for b in range(B):
                                last = nc.tensor.transpose(psum(u)[:, c, b * P:(b + 1) * P], src[:, b, c * P:(c + 1) * P], ident[:, :])
                        last.then_inc(filled.sem, 1)
                    elif stage in ("q", "k"):
                        u = (stage, s, l)
                        took(("T", s, "0" if l == 0 else l))
                        enter(u)
                        W = w[f"{stage}{l}"]
                        for m in range(C):
                            for c in range(C):
                                last = three(half(u, m), lambda p: W[:, p, c, m * P:(m + 1) * P], lambda p: X[:, p, c, :], c == 0, c == C - 1)
                        last.then_inc(filled.sem, 1)
                    elif stage == "v":
                        u = ("v", s, l)
                        enter(u)
                        rows_out(u, X, w[f"v{l}"]).then_inc(filled.sem, 1)
                    elif stage == "heads":
                        if i < B:
                            u = ("S", s, l, i)
                            if i == 0:
                                took(("q", s, l))
                            pe.wait_ge(*kD_in[i % 2].at(body, (s, l, i)))
                            enter(u)
                            for c in range(C):
                                last = three(half(u, c), lambda p: qT[:, p, c, i * P:(i + 1) * P],
                                             lambda p: kD[i % 2][:, p, c].rearrange("p h k -> p (h k)"), True, True)
                            last.then_inc(filled.sem, 1)
                        if i >= 2:
                            b = i - 2
                            u = ("O", s, l, b)
                            if b == 0:
                                pe.wait_ge(*v_ready.at(body, (s, l)))
                            took(("P", s, l, b))
                            enter(u)
                            for h in range(H):
                                terms = [(1, 1), (1, 0), (0, 2), (0, 1), (0, 0)]
                                for n, (pp, vp) in enumerate(terms):
                                    last = mm(psum(u)[:, 0, h * HD:(h + 1) * HD], p16[:, pp, h, :], v[:, vp, b, h * HD:(h + 1) * HD],
                                              start=n == 0, stop=n == len(terms) - 1)
                            last.then_inc(filled.sem, 1)
                        if 1 <= i <= B:
                            b = i - 1
                            u = ("P", s, l, b)
                            pe.wait_ge(*exp_ready.at(body, (s, l, b)))
                            enter(u)
                            for h in range(H):
                                last = nc.tensor.transpose(psum(u)[:, h // HC, h % HC * P:(h % HC + 1) * P], e[:, b % 2, h, :], ident[:, :])
                            last.then_inc(filled.sem, 1)
                    elif stage == "out_proj":
                        u = ("o", s, l)
                        took(("T", s, f"{l}a") if l in (0, 3) else ("X", s, l))
                        enter(u)
                        rows_out(u, X, w[f"o{l}"]).then_inc(filled.sem, 1)
                    elif stage == "mlp":
                        if i >= 2:
                            j, y = i - 2, ("y", s, l)
                            pe.wait_ge(*h_ready.at(body, (s, j)))
                            if j == 0:
                                enter(y)
                            for b in range(B):
                                last = three(psum(y)[:, b // 2, b % 2 * D:(b % 2 + 1) * D], lambda p: hT[j % 2][:, p, b * P:(b + 1) * P],
                                             lambda p: w["w2"][:, p, j, :], j == 0 and b % 2 == 0, j == FT - 1, skip_group_check=True)
                            if j == FT - 1:
                                last.then_inc(y_done.sem, 1)
                        if i < FT:
                            u = ("h", s, l, i)
                            if i == 0:
                                took(("T", s, "0m"))
                            enter(u)
                            for c in range(C):
                                last = three(half(u, 0), lambda p: w["w1"][:, p, c, i * P:(i + 1) * P], lambda p: X[:, p, c, :],
                                             c == 0, c == C - 1)
                            last.then_inc(filled.sem, 1)
                    elif stage == "qk1":
                        u = ("qk", s, l)
                        took(("T", s, l))
                        enter(u)
                        if l == 4:
                            outs = [(w["q4"], m * P, m) for m in range(C)]
                        else:
                            outs = [(w[f"q{l}"], 0, 0), (w[f"k{l}"], 0, 1)]
                        for W, f, m in outs:
                            for c in range(C):
                                last = three(half(u, m), lambda p: W[:, p, c, f:f + P], lambda p: X[:, p, c, :], c == 0, c == C - 1)
                        last.then_inc(filled.sem, 1)
                    elif stage == "S1":
                        u = ("S", s, l)
                        took(("qk", s, l))
                        if l == 4:
                            pe.wait_ge(*full_taken.at(body, (s, 4)))
                        enter(u)
                        q = xn[s][:].rearrange("p b d -> p (b d)")
                        for b in range(B):
                            g = slice(b * P, (b + 1) * P)
                            pairs = [(q[:, 0:R][:, g], q[:, R:2 * R][:, g])] if l != 4 else \
                                    [(q[:, c * R:(c + 1) * R][:, g], xT_full[:, c, g]) for c in range(C)]
                            for n, (a, k) in enumerate(pairs):
                                last = mm(psum(u)[:, 0, g], a, k, start=n == 0, stop=n == len(pairs) - 1)
                        last.then_inc(filled.sem, 1)
                    elif stage == "P1":
                        u = ("P", s, l)
                        pe.wait_ge(*p_ready.at(body, (s, l)))
                        enter(u)
                        for b in range(B):
                            last = nc.tensor.transpose(psum(u)[:, 0, b * P:(b + 1) * P], e1[:, 0, b, :], ident[:, :])
                        last.then_inc(filled.sem, 1)
                    elif stage == "X1":
                        u = ("X", s, l)
                        took(("P", s, l))
                        enter(u)
                        for c in range(C):
                            for b in range(B):
                                last = mm(psum(u)[:, c, b * P:(b + 1) * P], x[s][:, b, c * P:(c + 1) * P], e1[:, 1, b, :], start=True, stop=True)
                        last.then_inc(filled.sem, 1)

            run(first, 0)
            with pe.Fori(0, steps - 1) as it:
                run(loop, it)
            run(last_, 0)

        @block.scalar
        def _(act):
            activation = nc.scalar.activation
            pro_loads = [0, 0]
            act.wait_ge(par_in, 16 * n_par)
            for j, (name, src, kt, n, scale) in enumerate(jobs):
                pro_loads[j % 2] += 16 * (2 if isinstance(src, tuple) else 1)
                act.wait_ge(w_in[j % 2], pro_loads[j % 2])
                if isinstance(src, tuple):
                    act.wait_ge(w_mm, mm_rank[j] + 1)
                    last = activation(w[name][:, 0], slot[mm_rank[j] % SLOTS][:, :, 0:D], ACT.Copy, scale=scale or 1.0)
                elif isinstance(scale, str):
                    if j == 0:
                        act.wait_ge(w_col, 1)
                    col = ln1_gs if scale == "ln1_gs" else cols[scale][0]
                    for c in range(kt):
                        last = activation(w[name][:, 0, c], staging(j)[:, c], ACT.Copy, scale=col[:, c:c + 1])
                else:
                    last = activation(w[name][:, 0], staging(j), ACT.Copy, scale=scale or 1.0)
                last.then_inc(w_hi, 1)
            act.wait_ge(w_lo, JN)
            act.wait_ge(w_bias, 2)


            def run(body, it):
                def hi(u, dst):
                    act.wait_ge(*filled.at(body, u))
                    activation(dst, psum(u)[:, :, :], ACT.Copy).then_inc(hi_taken.sem, 1)

                def keys_gone():
                    for n in range(2):
                        act.wait_ge(*kD_in[n].so_far(body))

                for stage, s, l, i in body.walk(it):
                    if stage == "to_T":
                        u = ("T", s, l)
                        hi(u, xT[s][:, 0])
                        if l == 4:
                            keys_gone()
                            activation(xT_full, psum(u)[:, :, :], ACT.Copy).then_inc(full_taken.sem, 1)
                    elif stage in ("q", "k"):
                        u = (stage, s, l)
                        dst = qT[:, 0] if stage == "q" else kT[:, 0].bitcast(F32R)
                        act.wait_ge(*filled.at(body, u))
                        if stage == "k":
                            keys_gone()
                        for c in range(C):
                            last = activation(dst[:, c], psum(u)[:, c, :], ACT.Identity, bias=cols[f"b{stage}{l}"][0][:, c:c + 1])
                        last.then_inc(hi_taken.sem, 1)
                    elif stage == "v":
                        hi(("v", s, l), v[:, 0].rearrange("p (a b) d -> p a (b d)", a=2))
                    elif stage == "heads":
                        if i < B:
                            act.wait_ge(*scores_ready.at(body, (s, l, i)))
                            for h in range(H):
                                last = activation(e[:, i % 2, h, :], e[:, i % 2, h, :], ACT.Exp, bias=neg_max[:, i % 2, h:h + 1],
                                                  accum_out=total[:, i % 2, h:h + 1])
                            last.then_inc(exp_ready.sem, 1)
                        if 1 <= i <= B:
                            hi(("P", s, l, i - 1), p16[:, 0].rearrange("p (a h) k -> p a (h k)", a=2))
                    elif stage == "mlp" and i < FT:
                        u = ("h", s, l, i)
                        act.wait_ge(*filled.at(body, u))
                        if i >= 2:
                            act.wait_ge(*h_ready.at(body, (s, i - 2)))
                        activation(h32[:, i % 2, :], psum(u)[:, 0, :], ACT.Gelu, bias=cols["b1"][0][:, i:i + 1]).then_inc(taken[slot_of(u)].sem, 1)
                        act.wait_ge(*taken[slot_of(u)].at(body, u))
                        activation(hT[i % 2][:, 0], h32[:, i % 2, :], ACT.Copy).then_inc(hi_taken.sem, 1)
                    elif stage == "qk1":
                        u = ("qk", s, l)
                        act.wait_ge(*filled.at(body, u))
                        dst = xn[s][:].rearrange("p (m b) d -> p m (b d)", m=2)
                        if l == 4:
                            last = activation(dst, psum(u)[:, :, :], ACT.Copy)
                        else:
                            activation(dst[:, 0], psum(u)[:, 0, :], ACT.Identity, bias=cols[f"bq{l}"][0][:, 0:1])
                            last = activation(dst[:, 1], psum(u)[:, 1, :], ACT.Identity, bias=cols[f"bk{l}"][0][:, 0:1])
                        last.then_inc(taken[slot_of(u)].sem, 1)
                    elif stage == "S1":
                        act.wait_ge(*scores_ready.at(body, (s, l)))
                        for b in range(B):
                            last = activation(e1[:, 0, b, :], e1[:, 0, b, :], ACT.Exp, bias=neg_max[:, 2, b:b + 1],
                                              accum_out=total[:, 2, b:b + 1])
                        last.then_inc(exp_ready.sem, 1)
                    elif stage == "P1":
                        u = ("P", s, l)
                        act.wait_ge(*filled.at(body, u))
                        activation(e1[:, 1].rearrange("p b k -> p (b k)"), psum(u)[:, 0, :], ACT.Copy).then_inc(taken[slot_of(u)].sem, 1)
                    elif stage == "X1":
                        hi(("X", s, l), xT[s][:, 0])

            run(first, 0)
            with act.Fori(0, steps - 1) as it:
                run(loop, it)
            run(last_, 0)

        @block.vector
        def _(dve):
            V = nc.vector
            pro = [0]

            def link_pro(ins):
                pro[0] += 1
                ins.then_inc(dve_pro, 1)
                dve.wait_ge(dve_pro, pro[0])

            dve.wait_ge(par_in, 16 * n_par)
            dve.wait_ge(one_made, 4)
            V.tensor_scalar(ln1_gs[:, :], cols["ln1_g"][0][:, :], scale_hd, None, ALU.mult).then_inc(w_col, 1)
            for name in ("bq1", "bq2"):
                link_pro(V.tensor_scalar(cols[name][0][:, :], cols[name][0][:, :], scale_dk, None, ALU.mult))
            link_pro(V.tensor_scalar(cols["bq3"][0][:, :], cols["bq3"][0][:, :], scale_hd, None, ALU.mult))

            def widen(col):
                for c in range(C):
                    last = V.tensor_scalar(bv_wide[:, c, :], ident[:, :], 0.0, col[:, c:c + 1], ALU.mult, ALU.add)
                last.then_inc(w_col, 1)

            for j, (name, src, kt, n, scale) in enumerate(jobs):
                if j in mm_rank:
                    dve.wait_ge(w_mm, mm_rank[j] + 1)
                    ps = slot[mm_rank[j] % SLOTS]
                    if name in ("q0", "k0", "v0", "w1"):
                        col = cols["b1" if name == "w1" else f"b{name}"][0]
                        link_pro(V.tensor_tensor(col[:, :], ps[:, 0, 0:n // P], col[:, :], ALU.add))
                        if name == "q0":
                            link_pro(V.tensor_scalar(col[:, :], col[:, :], scale_hd, None, ALU.mult))
                    if name in ("o0", "o3"):
                        row = rows[f"b{name}"][0]
                        V.tensor_tensor(row[:, :], ps[:, 0, 0:D], row[:, :], ALU.add).then_inc(w_bias, 1)
                dve.wait_ge(w_hi, j + 1)
                high = w[name][:, 0].bitcast(F32)
                if isinstance(src, tuple):
                    last = V.scalar_tensor_tensor(out=w[name][:, 1], in0=slot[mm_rank[j] % SLOTS][:, :, 0:D], scalar=scale or 1.0,
                                                  in1=high, op0=ALU.mult, op1=ALU.subtract)
                elif isinstance(scale, str):
                    col = ln1_gs if scale == "ln1_gs" else cols[scale][0]
                    for c in range(kt):
                        last = V.scalar_tensor_tensor(out=w[name][:, 1, c], in0=staging(j)[:, c], scalar=col[:, c:c + 1],
                                                      in1=high[:, c], op0=ALU.mult, op1=ALU.subtract)
                else:
                    last = V.scalar_tensor_tensor(out=w[name][:, 1], in0=staging(j), scalar=scale or 1.0, in1=high,
                                                  op0=ALU.mult, op1=ALU.subtract)
                last.then_inc(w_lo, 1)
                if name in ("v0", "v3"):
                    if name == "v3":
                        dve.wait_ge(w_bias, 1)
                    widen(cols[f"b{name}"][0])

            def run(body, it):
                body.it = it
                chain = Chain(dve, dve_step)
                chain.start(body)
                link = chain.link

                def done(instruction, signal, key):
                    instruction.then_inc(signal.sem, 1)
                    dve.wait_ge(*signal.at(body, key))

                def took(instruction, u):
                    done(instruction, taken[slot_of(u)], u)

                def lo(u, dst, high):
                    dve.wait_ge(*hi_taken.at(body, u))
                    took(V.tensor_tensor(dst, psum(u)[:, :, :], high, ALU.subtract), u)

                def scores(u, e_, bias_, n, heads_, key):
                    took(V.tensor_tensor(e_, psum(u)[:, :, :].rearrange("p a n -> p (a n)")[:, 0:heads_ * P].rearrange("p (h k) -> p h k", k=P),
                                         bias_, ALU.add), u)
                    done(V.tensor_reduce(out=neg_max[:, n, 0:heads_], in_=e_, op=ALU.max, axis=AX.X, negate=True), scores_ready, key)

                for stage, s, l, i in body.walk(it):
                    x_banks = x[s][:].rearrange("p (a b) d -> p a (b d)", a=2)
                    if stage == "load":
                        dve.wait_ge(*adj_in.at(body, (s, l)))
                        dve.wait_ge(*filled.so_far(body))
                        a, d, m = (y[:, :, :] if y is not xn[s] else y[:, 0:2].rearrange("p a (b k) -> p (a b) k", k=P)
                                   for y in (adj[s], bias[s], xn[s]))
                        link(V.tensor_scalar(d, a, 0.1, None, ALU.mult))
                        link(V.tensor_tensor(d, d, a, ALU.mult))
                        link(V.tensor_scalar(m, a, 0.0, None, ALU.is_gt))
                        link(V.tensor_tensor(d, d, m, ALU.mult))
                        link(V.tensor_scalar(m, m, 1.0, -MASKED, ALU.subtract, ALU.mult))
                        link(V.tensor_tensor(d, d, m, ALU.add))
                    elif stage == "norm_stat":
                        st, mu, gp, va = stats[s], mean[s], gap[s], var[s]
                        if l == 0:
                            dve.wait_ge(*x_in.at(body, (s, 0)))
                        for b in range(B):
                            last = V.bn_stats(st[:, b, :], x[s][:, b, :])
                        link(last)
                        even_mean, even_m2, odd_mean, odd_m2 = (st[:, :, n] for n in (1, 2, 4, 5))
                        V.tensor_tensor(mu[:, :], even_mean, odd_mean, ALU.add)
                        V.tensor_tensor(gp[:, :], even_mean, odd_mean, ALU.subtract)
                        link(V.tensor_tensor(va[:, :], even_m2, odd_m2, ALU.add))
                        V.tensor_scalar(mu[:, :], mu[:, :], 0.5, None, ALU.mult)
                        V.scalar_tensor_tensor(out=gp[:, :], in0=gp[:, :], scalar=0.25, in1=gp[:, :], op0=ALU.mult, op1=ALU.mult)
                        link(V.tensor_scalar(va[:, :], va[:, :], 1.0 / D, EPS, ALU.mult, ALU.add))
                        done(V.tensor_tensor(va[:, :], va[:, :], gp[:, :], ALU.add), var_ready, (s, l))
                    elif stage == "norm_apply":
                        dve.wait_ge(*rstd_ready.at(body, (s, l)))
                        if l in (0, "mid"):
                            for b in range(B):
                                last = V.tensor_scalar(xn[s][:, b, :], x[s][:, b, :], mean[s][:, b:b + 1], rstd[s][:, b:b + 1],
                                                       ALU.subtract, ALU.mult)
                        else:
                            g, b_ = rows[f"g{l}"][0], rows[f"b_{l}"][0]
                            for b in range(B):
                                last = V.scalar_tensor_tensor(out=x[s][:, b, :], in0=x[s][:, b, :], scalar=mean[s][:, b:b + 1], in1=g[:, :],
                                                              op0=ALU.subtract, op1=ALU.mult)
                            link(last)
                            for b in range(B):
                                last = V.scalar_tensor_tensor(out=x[s][:, b, :], in0=x[s][:, b, :], scalar=rstd[s][:, b:b + 1], in1=b_[:, :],
                                                              op0=ALU.mult, op1=ALU.add)
                        done(last, rows_ready, (s, l))
                    elif stage == "to_T":
                        if l == 1:
                            link(V.tensor_scalar(bias[s][:, :, :], adj[s][:, :, :], 0.0, MASKED, ALU.is_equal, ALU.mult))
                        if l == 4:
                            dve.wait_ge(*full_taken.at(body, (s, 4)))
                        lo(("T", s, l), xT[s][:, 1], xT[s][:, 0].bitcast(F32))
                    elif stage in ("q", "k"):
                        u = (stage, s, l)
                        dst, high = (qT[:, 1], qT[:, 0].bitcast(F32)) if stage == "q" else (kT[:, 1].bitcast(F32R), kT[:, 0])
                        dve.wait_ge(*hi_taken.at(body, u))
                        for c in range(C):
                            last = V.scalar_tensor_tensor(out=dst[:, c], in0=psum(u)[:, c, :], scalar=cols[f"b{stage}{l}"][0][:, c:c + 1],
                                                          in1=high[:, c], op0=ALU.add, op1=ALU.subtract)
                        took(last, u)
                    elif stage == "v":
                        part = [v[:, p].rearrange("p (a b) d -> p a (b d)", a=2) for p in range(3)]
                        rest = xn[s][:].rearrange("p (a b) d -> p a (b d)", a=2)
                        lo(("v", s, l), rest, part[0])
                        link(V.tensor_copy(part[1], rest))
                        done(V.tensor_tensor(part[2], rest, part[1], ALU.subtract), v_ready, (s, l))
                    elif stage == "heads":
                        if i < B:
                            u = ("S", s, l, i)
                            dve.wait_ge(*filled.at(body, u))
                            scores(u, e[:, i % 2], bias[s][:, i, :].unsqueeze(1).broadcast_to([P, H, P]), i % 2, H, (s, l, i))
                        if i >= 2:
                            b = i - 2
                            u = ("O", s, l, b)
                            dve.wait_ge(*filled.at(body, u))
                            took(V.tensor_tensor(xn[s][:, b, :].rearrange("p (h d) -> p h d", d=HD),
                                                 psum(u)[:, 0, 0:D].rearrange("p (h d) -> p h d", d=HD),
                                                 rinv[:, b % 2, :].unsqueeze(2).broadcast_to([P, H, HD]), ALU.mult), u)
                        if 1 <= i <= B:
                            b = i - 1
                            lo(("P", s, l, b), p16[:, 1].rearrange("p (a h) k -> p a (h k)", a=2),
                               p16[:, 0].rearrange("p (a h) k -> p a (h k)", a=2))
                            link(V.reciprocal(rinv[:, b % 2, :], total[:, b % 2, :]))
                    elif stage == "out_proj":
                        u = ("o", s, l)
                        if l in (0, 3, 4):
                            dve.wait_ge(*b_added.at(body, (s, l)))
                        dve.wait_ge(*filled.at(body, u))
                        took(V.tensor_tensor(x_banks, psum(u)[:, :, :], x_banks, ALU.add), u)
                    elif stage == "mlp":
                        if i < FT:
                            dve.wait_ge(*hi_taken.at(body, ("h", s, l, i)))
                            done(V.tensor_tensor(hT[i % 2][:, 1], h32[:, i % 2, :], hT[i % 2][:, 0].bitcast(F32), ALU.subtract), h_ready, (s, i))
                        if i == FT + 1:
                            u = ("y", s, l)
                            dve.wait_ge(*b_added.at(body, (s, "mid")))
                            dve.wait_ge(*y_done.at(body, (s, l)))
                            took(V.tensor_tensor(x_banks, psum(u)[:, :, :], x_banks, ALU.add), u)
                    elif stage == "S1":
                        u = ("S", s, l)
                        dve.wait_ge(*filled.at(body, u))
                        scores(u, e1[:, 0], bias[s][:, :, :], 2, B, (s, l))
                    elif stage == "P1":
                        dve.wait_ge(*exp_ready.at(body, (s, l)))
                        link(V.reciprocal(rinv[:, 2, 0:B], total[:, 2, 0:B]))
                        p = e1[:, 0]
                        r = rinv[:, 2, 0:B].unsqueeze(2).broadcast_to([P, B, P])
                        if l == 4:
                            done(V.tensor_tensor(p, p, r, ALU.mult), p_ready, (s, l))
                        else:
                            link(V.tensor_tensor(p, p, r, ALU.mult))
                            link(V.tensor_scalar(e1[:, 1], adj[s][:, :, :], 0.0, None, ALU.not_equal))
                            done(V.tensor_tensor(p, p, e1[:, 1], ALU.mult), p_ready, (s, l))
                    elif stage == "X1":
                        lo(("X", s, l), xT[s][:, 1], xT[s][:, 0].bitcast(F32))
                chain.end()

            run(first, 0)
            with dve.Fori(0, steps - 1) as it:
                run(loop, it)
            run(last_, 0)


LAYERED = {"L1_gnn_Wq": True, "L1_gnn_Wk": True, "L1_gnn_Wc": True, "L1_gnn_bq": False, "L1_gnn_bk": False,
           "L1_gnn_ln_g": False, "L1_gnn_ln_b": False}
COLUMNS = ("L0_gnn_ln1_g", "L0_gnn_ln1_b", "L0_gnn_ln2_g", "L0_gnn_ln2_b", "L0_gnn_bq", "L0_gnn_bk", "L0_gnn_bv", "L0_gnn_b1",
           "L1_gnn_bq0", "L1_gnn_bk0", "L1_gnn_bq1", "L1_gnn_bk1", "L2_gnn_bq", "L2_gnn_bk", "L2_gnn_bv")
TRANSPOSED = ("L3_gnn_Wq", "L3_gnn_Wk", "L3_gnn_Wv")


def laid_out(inputs):
    arrays = {}
    for name, a in inputs.items():
        a = np.asarray(a)
        if name in LAYERED:
            for n in range(a.shape[0]):
                arrays[f"{name}{'T' if LAYERED[name] else ''}{n}"] = np.ascontiguousarray(a[n].T)
        elif name in TRANSPOSED:
            arrays[f"{name}T"] = np.ascontiguousarray(a.T)
        else:
            arrays[name] = np.ascontiguousarray(a)
    for name in COLUMNS:
        arrays[name + "_col"] = np.ascontiguousarray(arrays.pop(name).reshape(-1, P).T)
    return arrays


def kernel(**inputs):
    import concourse.bacc as bacc
    from concourse.bass_utils import run_bass_kernel_spmd

    nc = bacc.Bacc("TRN2", target_bir_lowering=False, num_devices=1)
    arrays = laid_out(inputs)
    t = {n: nc.dram_tensor(f"in_{n}", a.shape, mybir.dt.from_np(a.dtype), kind="ExternalInput").ap() for n, a in arrays.items()}
    graphs = arrays["x"].shape[0]
    out = nc.dram_tensor("out", (graphs, P, D), F32, kind="ExternalOutput").ap()
    mk_kernel(nc, graphs // (B * STREAMS), t, out)
    r = run_bass_kernel_spmd(nc, [{f"in_{n}": a for n, a in arrays.items()}], core_ids=[0])
    return r.results[0]["out"]
```

```python
from contextlib import ExitStack

import numpy as np

import concourse.bass as bass
from concourse import mybir

F32 = mybir.dt.float32
F32R = mybir.dt.float32r
F16 = mybir.dt.float16
BF16 = mybir.dt.bfloat16
I32 = mybir.dt.int32
ALU = mybir.AluOpType
ACT = mybir.ActivationFunctionType
AX = mybir.AxisListType

P = 128
D = 256
C = D // P
B = 2
R = B * P
H = 8
HD = D // H
HC = P // HD
FF = 4 * D
FT = FF // P
DK = 128
EPS = 1e-5
MASKED = -1e30
STREAMS = 4
SLOTS = 7
N_ITEMS = B * C
N_TILES = FT // 2


COST = {
    "load": 2.0, "k_move": 3.0, "store": 0.5,
    "T": 0.5, "k": 1.4, "q": 1.4, "v": 2.24, "S": 0.7, "P": 0.5, "O": 1.0, "o": 1.4, "h": 1.4, "y": 1.4, "qk": 1.4,
    "S1": 0.7, "P1": 0.3, "X": 0.9,
    "apply": 0.7, "T_hi": 0.6, "T_full": 0.6, "k_hi": 0.7, "q_hi": 0.7, "v_hi": 0.6, "v_mid": 0.6, "exp": 0.8, "P_hi": 0.6,
    "gelu": 0.7, "h_hi": 0.6, "qk_out": 0.7, "exp1": 0.4, "P1_out": 0.4, "X_hi": 0.6,
    "bias": 1.5, "edges": 0.8, "stats": 1.2, "T_lo": 0.6, "k_lo": 0.7, "q_lo": 0.42, "v_rest": 0.6, "mask": 1.3, "P_lo": 0.6,
    "O_out": 0.3, "o_add": 0.6, "y_add": 0.6, "mask1": 0.7, "p_norm": 0.8, "X_lo": 0.6,
    "rstd": 1.3, "affine": 2.4, "v_low": 1.2, "h_lo": 1.2, "add_row": 1.2,
}
HOP = 0.31
ITEM_GAP = 2.72
VALUES_AT = 2.8
TILE_GAP = 3.2
PAUSE = {"attention0": 0, "mlp": 4.59, "1": 5.0, "2": 3.77, "attention3": 0.0, "4": 1.08}
LENGTH = 188.51
DVE_LINKS = {"bias": 3, "stats": 3, "edges": 2, "p_norm": 2}
POOL_LINKS = {"rstd": 1, "affine": 1}


def path(s):
    out = []

    def chain(t, names, l, i=0):
        for name in names.split():
            out.append((t, (name, s, l, i)))
            t += COST[name] + HOP
        return t

    def normalised(t, l):
        return chain(t, "stats rstd apply" if l in ("0", "mid") else "stats rstd apply affine", l)

    def attention(t, l):
        t += PAUSE[f"attention{l}"]
        keys = chain(t, "k k_hi k_lo k_move", l)
        queries = chain(t + 1.4, "q q_hi q_lo", l)
        chain(t + VALUES_AT, "v v_hi v_rest v_mid v_low", l)
        t = max(keys, queries)
        for j in range(N_ITEMS):
            end = chain(t + j * ITEM_GAP, "S mask exp P P_hi P_lo O O_out", l, j)
        return end

    def one_head(t, l):
        t = chain(t + PAUSE[str(l)], "T T_hi T_full T_lo qk qk_out" if l == 4 else "T T_hi T_lo qk qk_out", l)
        t = chain(t, "S1 mask1 exp1 p_norm P1 P1_out X X_hi X_lo", l)
        if l == 4:
            chain(t - 1.5, "add_row", l)
        return normalised(chain(t, "o o_add", l), l)

    chain(0.0, "load", 0)
    t = normalised(chain(2.0, "bias", 0), "0")
    chain(t + 0.2, "add_row", "0")
    t = attention(chain(t, "T T_hi T_lo", "0"), 0)
    t = chain(t, "T T_hi T_lo", "0a")
    t = normalised(chain(t, "o o_add", 0), "mid")
    chain(t + 0.2, "add_row", "mid")
    t = chain(t + PAUSE["mlp"], "T T_hi T_lo", "0m")
    chain(t, "edges", 0)
    for j in range(N_TILES):
        end = chain(t + j * TILE_GAP, "h gelu h_hi h_lo y", 0, j)
    t = chain(end, "y_add", 0)
    t = one_head(one_head(t, 1), 2)
    t = chain(t, "T T_hi T_lo", 3)
    chain(t + 0.2, "add_row", 3)
    t = attention(t, 3)
    t = chain(t, "T T_hi T_lo", "3a")
    t = normalised(chain(t, "o o_add", 3), 3)
    t = chain(one_head(t, 4), "store", 4)
    assert t <= LENGTH
    return sorted(out, key=lambda x: x[0])


TAKER = {"T": "T_lo", "k": "k_lo", "q": "q_lo", "v": "v_rest", "S": "mask", "P": "P_lo", "O": "O_out", "o": "o_add", "h": "gelu",
         "qk": "qk_out", "S1": "mask1", "P1": "P1_out", "X": "X_lo"}
TAKES = {taker: name for name, taker in TAKER.items()}


def taker(op):
    return (TAKER[op[0]], *op[1:])


def ordered():
    ways = [path(s) for s in range(STREAMS)]
    by_time = sorted(((t + s * LENGTH / STREAMS) % LENGTH, s, n, op, t + s * LENGTH / STREAMS >= LENGTH)
                     for s, way in enumerate(ways) for n, (t, op) in enumerate(way))
    tail_of = {op: tail for _, _, _, op, tail in by_time}
    left = {}
    for _ in range(3):
        waiting, out, holds, done, n = list(by_time), [], dict(left), set(), 0
        done.update(taker(u) for u in left.values() if tail_of[taker(u)] == tail_of[u])
        while waiting:
            late = set()
            for k, (_, s, _, op, _) in enumerate(waiting):
                unit = holds.get(n % SLOTS) if op[0] in TAKER else None
                if s not in late and (unit is None or taker(unit) in done):
                    break
                late.add(s)
            _, _, _, op, tail = waiting.pop(k)
            out.append((op, tail))
            done.add(op)
            if op[0] in TAKER:
                holds[n % SLOTS] = op
                n += 1
        fits, left = left == holds, holds
    assert fits
    return out, left


class Body:

    def __init__(self, ops, before):
        self.ops, self.before = ops, before
        self.it, self.now = 0, 0

    def walk(self, it=0):
        self.it = it
        for self.now, op in enumerate(self.ops):
            yield op


class Signal:

    START = 1

    def __init__(self, sem, signals, bodies, unit=1):
        self.sem, self.unit = sem, unit
        self.rank, self.place, self.size = {}, {}, {}
        for body in bodies:
            found = [(n, op) for n, op in enumerate(body.ops) if signals(op)]
            self.rank[body] = {op: k for k, (_, op) in enumerate(found)}
            self.place[body] = {op: n for n, op in found}
            self.size[body] = len(found) * unit

    def before(self, body):
        base = sum(self.size[b] * times for b, times in body.before) + self.START
        return self.sem, body.it * self.size[body] + base

    def at(self, body, op):
        sem, base = self.before(body)
        if op not in self.place[body] or self.place[body][op] > body.now:
            return sem, base
        return sem, base + (self.rank[body][op] + 1) * self.unit


class Chain:

    def __init__(self, engine, steps, links):
        self.engine, self.steps, self.links = engine, steps, links

    def start(self, body):
        self.body, self.n = body, 0

    def link(self, instruction):
        sem, base = self.steps.before(self.body)
        instruction.then_inc(sem, 1)
        self.n += 1
        self.engine.wait_ge(sem, base + self.n)

    def end(self):
        assert self.n == sum(self.links.get(op[0], 0) for op in self.body.ops)


def mk_kernel(nc, steps, t, out):
    scale_hd = float(1.0 / np.sqrt(HD))
    scale_dk = float(1.0 / np.sqrt(DK))
    scale_d = float(1.0 / np.sqrt(D))
    ctx = ExitStack()
    with ctx:
        def sb(name, shape, dt):
            return ctx.enter_context(nc.sbuf_tensor(name, shape, dt))

        def sem(name):
            return ctx.enter_context(nc.semaphore(name))

        jobs = [
            ("q0", "L0_gnn_wq", C, D, "ln1_gs"), ("k0", "L0_gnn_wk", C, D, "ln1_g"), ("v0", "L0_gnn_wv", C, D, "ln1_g"),
            ("o0", "L0_gnn_wo", C, D, None), ("w1", "L0_gnn_w1", C, FF, "ln2_g"), ("w2", "L0_gnn_w2", FT, D, None),
            ("q1", "L1_gnn_WqT0", C, DK, scale_dk), ("k1", "L1_gnn_WkT0", C, DK, None), ("o1", "L1_gnn_WcT0", C, D, None),
            ("q2", "L1_gnn_WqT1", C, DK, scale_dk), ("k2", "L1_gnn_WkT1", C, DK, None), ("o2", "L1_gnn_WcT1", C, D, None),
            ("q3", "L2_gnn_Wq", C, D, scale_hd), ("k3", "L2_gnn_Wk", C, D, None), ("v3", "L2_gnn_Wv", C, D, None),
            ("o3", "L2_gnn_Wo", C, D, None),
            ("q4", ("L3_gnn_WqT", "L3_gnn_WkT"), C, D, scale_d), ("o4", ("L3_gnn_WvT", "L3_gnn_Wo"), C, D, None),
        ]
        w = {j[0]: sb(f"w_{j[0]}", [P, 2, j[2], j[3]], F32R) for j in jobs}

        cols = {}
        for name, src, n in (
            ("ln1_g", "L0_gnn_ln1_g", C), ("ln1_b", "L0_gnn_ln1_b", C), ("ln2_g", "L0_gnn_ln2_g", C),
            ("ln2_b", "L0_gnn_ln2_b", C), ("bq0", "L0_gnn_bq", C), ("bk0", "L0_gnn_bk", C), ("bv0", "L0_gnn_bv", C),
            ("b1", "L0_gnn_b1", FT), ("bq1", "L1_gnn_bq0", 1), ("bk1", "L1_gnn_bk0", 1), ("bq2", "L1_gnn_bq1", 1),
            ("bk2", "L1_gnn_bk1", 1), ("bq3", "L2_gnn_bq", C), ("bk3", "L2_gnn_bk", C), ("bv3", "L2_gnn_bv", C),
        ):
            cols[name] = (sb(f"c_{name}", [P, n], F32), src)
        ln1_gs = sb("ln1_gs", [P, C], F32)
        rows = {}
        for name, src in (
            ("bo0", "L0_gnn_bo"), ("b2", "L0_gnn_b2"), ("bo3", "L2_gnn_bo"), ("bo4", "L3_gnn_bo"),
            ("g1", "L1_gnn_ln_g0"), ("b_1", "L1_gnn_ln_b0"), ("g2", "L1_gnn_ln_g1"), ("b_2", "L1_gnn_ln_b1"),
            ("g3", "L2_gnn_gamma"), ("b_3", "L2_gnn_beta"), ("g4", "L3_gnn_gamma"), ("b_4", "L3_gnn_beta"),
        ):
            rows[name] = (sb(f"r_{name}", [P, D], F32), src)
        ident = sb("ident", [P, P], F32)
        started = sb("started", [P, 64], mybir.dt.uint8)
        minus_half = sb("minus_half", [P, B], F32)
        one_each = sb("one_each", [P, B], F32)

        x = [sb(f"x{s}", [P, B, D], F32) for s in range(STREAMS)]
        xn = [sb(f"xn{s}", [P, B, D], F32) for s in range(STREAMS)]
        xT = [sb(f"xT{s}", [P, 2, C, R], F32R) for s in range(STREAMS)]
        adj = [sb(f"adj{s}", [P, B, P], I32) for s in range(STREAMS)]
        bias = [sb(f"bias{s}", [P, B, P], F32) for s in range(STREAMS)]
        qT = sb("qT", [P, 2, C, R], F32R)
        v = sb("v", [P, B, H, 3, HD], BF16)
        v_parts = v[:].rearrange("p b h a d -> p a (b h) d")
        kT = sb("kT", [P, 2, C, R], F32)
        kD = sb("kD", [P, 2, C, B, HC, P], F32R)
        e = sb("e", [P, B, C, HC, P], F32)
        p16 = sb("p16", [P, B, C, 2, HC, P], F16)
        h32 = sb("h32", [P, 2, 2, R], F32)
        hT = [sb(f"hT{n}", [P, 2, 2, R], F32R) for n in range(2)]
        area = sb("area", [P, 2 * H * P], F32)
        n1 = 2 * B * P
        e1 = {l: area[:, n * n1:(n + 1) * n1].rearrange("p (a b k) -> p a b k", a=2, b=B)
              for n, l in enumerate((1, 2, 4))}
        xT_full = area[:, 3 * n1:3 * n1 + C * R].rearrange("p (c r) -> p c r", c=C)
        bv_wide = xn[0][:, 0, :].rearrange("p (c k) -> p c k", c=C)
        stats = [sb(f"stats{s}", [P, B, 6], F32) for s in range(STREAMS)]
        shift = [sb(f"shift{s}", [P, B], F32) for s in range(STREAMS)]
        gap = [sb(f"gap{s}", [P, B], F32) for s in range(STREAMS)]
        var = [sb(f"var{s}", [P, B], F32) for s in range(STREAMS)]
        rstd = [sb(f"rstd{s}", [P, B], F32) for s in range(STREAMS)]
        has_edge = [sb(f"has_edge{s}", [P, B], F32) for s in range(STREAMS)]
        neg_max = sb("neg_max", [P, B, H], F32)
        total = sb("total", [P, B, H], F32)
        rinv = sb("rinv", [P, B, H], F32)
        neg_max1, total1, rinv1 = ([sb(f"{name}1_{s}", [P, B], F32) for s in range(STREAMS)] for name in ("neg_max", "total", "rinv"))

        bank = [ctx.enter_context(nc.psum_tensor(f"bank{n}", [P, 512], F32)) for n in range(SLOTS + 1)]

        order, left = ordered()
        first = Body([op for op, tail in order if not tail], [])
        loop = Body([op for op, _ in order], [(first, 1)])
        last_ = Body([op for op, tail in order if tail], [(first, 1), (loop, steps - 1)])
        bodies = [first, loop, last_]
        tails = {op for op, tail in order if tail}
        units = [op for op in loop.ops if op[0] in TAKER]
        bank_of = {u: n % SLOTS for n, u in enumerate(units)}
        held_before = {}
        for body in bodies:
            held = dict(left) if body is not first else {}
            for u in body.ops:
                if u in bank_of:
                    held_before[body, u] = held.get(bank_of[u])
                    held[bank_of[u]] = u
            assert body is last_ or held == left

        def flat(u, n=512):
            return bank[bank_of[u]][:, 0:n]

        def by_head(u):
            return flat(u).rearrange("p (h k) -> p h k", h=HC)

        def by_feature(u):
            return flat(u).rearrange("p (g d) -> p g d", d=HD)

        def halves(u):
            return flat(u).rearrange("p (c r) -> p c r", c=C)

        def y_sum():
            return bank[SLOTS][:, :]

        def signal(name, names, unit=1):
            return Signal(sem(name), lambda op: op[0] in names.split(), bodies, unit)

        def of_stream(name, names, s, unit):
            return Signal(sem(name), lambda op: op[0] in names.split() and op[1] == s, bodies, unit)

        filled = signal("filled", " ".join(TAKER) + " y")
        taken = [Signal(sem(f"taken{n}"), lambda op, n=n: op[0] in TAKES and bank_of[(TAKES[op[0]], *op[1:])] == n, bodies) for n in range(SLOTS)]
        taken.append(signal("y_taken", "y_add"))
        hi_taken = signal("hi_taken", "T_hi T_full k_hi q_hi v_hi P_hi h_hi X_hi")
        x_in = [of_stream(f"x_in{s}", "load", s, 16) for s in range(STREAMS)]
        adj_in = [of_stream(f"adj_in{s}", "load", s, 16) for s in range(STREAMS)]
        stored = [of_stream(f"stored{s}", "store", s, 16) for s in range(STREAMS)]
        keys_in = signal("keys_in", "k_move", 16 * HC)
        var_ready = signal("var_ready", "stats")
        rstd_ready = signal("rstd_ready", "rstd")
        xn_ready = signal("xn_ready", "apply")
        rows_ready = signal("rows_ready", "affine")
        row_added = signal("row_added", "add_row")
        scores_ready = signal("scores_ready", "mask mask1")
        exp_ready = signal("exp_ready", "exp exp1")
        p_ready = signal("p_ready", "p_norm")
        heads_ready = signal("heads_ready", "O_out")
        v2_ready = signal("v2_ready", "v_mid")
        v_ready = signal("v_ready", "v_low")
        h_ready = signal("h_ready", "h_lo")
        dve_step = signal("dve_step", " ".join(DVE_LINKS))
        pool_step = signal("pool_step", " ".join(POOL_LINKS))
        for steps_, links in ((dve_step, DVE_LINKS), (pool_step, POOL_LINKS)):
            for body in bodies:
                steps_.size[body] = sum(links.get(op[0], 0) for op in body.ops)
        signals = [filled, *taken, hi_taken, *x_in, *adj_in, *stored, keys_in, var_ready, rstd_ready, xn_ready, rows_ready, row_added,
                   scores_ready, exp_ready, p_ready, heads_ready, v2_ready, v_ready, h_ready, dve_step, pool_step]
        pool_pro = sem("pool_pro")
        stages_in = [area[:, :], e[:].rearrange("p b c h k -> p (b c h k)"), kT[:].rearrange("p a c r -> p (a c r)"),
                     h32[:].rearrange("p a m r -> p (a m r)")]
        N_STAGES = len(stages_in)

        par_in, one_made = sem("par_in"), sem("const_made")
        w_in = [sem(f"w_in{n}") for n in range(N_STAGES)]
        w_mm, w_hi, w_lo, w_col, w_bias = sem("w_mm"), sem("w_hi"), sem("w_lo"), sem("w_col"), sem("w_bias")
        dve_pro = sem("dve_pro")
        n_par = len(cols) + len(rows)
        JN = len(jobs)

        def staging(j):
            base = stages_in[j % N_STAGES]
            _, _, kt, n, _ = jobs[j]
            return base[:, 0:kt * n].rearrange("p (k n) -> p k n", k=kt)

        def staging2(j):
            base = stages_in[j % N_STAGES]
            return base[:, C * D:2 * C * D].rearrange("p (k n) -> p k n", k=C)

        MM_JOBS = [j for j, jb in enumerate(jobs) if jb[0] in ("q0", "k0", "v0", "o0", "w1", "o3", "q4", "o4")]
        mm_rank = {j: n for n, j in enumerate(MM_JOBS)}

        block = ctx.enter_context(nc.Block())

        @block.sync
        def _(sp):
            for name, (dst, src) in cols.items():
                sp.dma_start(dst[:, :], t[src + "_col"]).then_inc(par_in, 16)
            for j, (name, src, kt, n, _) in enumerate(jobs):
                if j >= N_STAGES:
                    sp.wait_ge(w_lo, j - N_STAGES + 1)
                    sp.wait_ge(w_hi, j - N_STAGES + 1)
                if isinstance(src, tuple):
                    sp.dma_start(staging(j), t[src[0]].rearrange("(k p) n -> p k n", p=P)).then_inc(w_in[j % N_STAGES], 16)
                    sp.dma_start(staging2(j), t[src[1]].rearrange("(k p) n -> p k n", p=P)).then_inc(w_in[j % N_STAGES], 16)
                else:
                    sp.dma_start(staging(j), t[src].rearrange("(k p) n -> p k n", p=P)).then_inc(w_in[j % N_STAGES], 16)
            x_v = t["x"].rearrange("(i b) n f -> i n b f", b=B)
            adj_v = t["adj"].rearrange("(i b) n m -> i n b m", b=B)
            out_v = out.rearrange("(i b) n f -> i n b f", b=B)

            def run(body, it):
                def group(op):
                    s = op[1]
                    if body is first:
                        return s
                    if body is last_:
                        return (steps - 1) * STREAMS + s
                    return it * STREAMS + s + (0 if op in tails else STREAMS)

                for op in body.walk(it):
                    name, s, l, i = op
                    if name == "load":
                        sp.wait_ge(*stored[s].at(body, ("store", s, 4, 0)))
                        sp.dma_start(x[s][:, :, :], x_v[group(op)]).then_inc(x_in[s].sem, 16)
                        sp.dma_start(adj[s][:, :, :], adj_v[group(op)]).then_inc(adj_in[s].sem, 16)
                    elif name == "k_move":
                        k = ("k", s, l, 0)
                        sp.wait_ge(*taken[bank_of[k]].at(body, ("k_lo", s, l, 0)))
                        for h in range(HC):
                            q = slice(h * HD, (h + 1) * HD)
                            sp.dma_start(kD[q, :, :, :, h, :].bitcast(F32).rearrange("p a c b k -> p (a c b) k"),
                                         kT[q].rearrange("p a c (b k) -> p (a c b) k", b=B)).then_inc(keys_in.sem, 16)
                    elif name == "store":
                        sp.wait_ge(*rows_ready.at(body, ("affine", s, 4, 0)))
                        sp.dma_start(out_v[group(op)], x[s][:, :, :]).then_inc(stored[s].sem, 16)

            run(first, 0)
            with sp.Fori(0, steps - 1) as it:
                run(loop, it)
            run(last_, 0)
            last_.now = len(last_.ops)
            for s in range(STREAMS):
                sp.wait_ge(*stored[s].at(last_, ("store", s, 4, 0)))

        @block.gpsimd
        def _(pool):
            nc.gpsimd.memset(ident[:, :], 0.0).then_inc(pool_pro, 1)
            pool.wait_ge(pool_pro, 1)
            nc.gpsimd.affine_select(out=ident[:, :], in_=ident[:, :], compare_op=ALU.not_equal, fill=1.0, base=0,
                                    pattern=[[-1, P]], channel_multiplier=1).then_inc(one_made, 1)
            nc.gpsimd.memset(minus_half[:, :], -0.5).then_inc(one_made, 1)
            nc.gpsimd.memset(one_each[:, :], 1.0).then_inc(one_made, 1)
            nc.gpsimd.memset(kD[:].bitcast(F32), 0.0).then_inc(one_made, 1)
            for n, each in enumerate(signals):
                nc.gpsimd.memset(started[:, n:n + 1], 0).then_inc(each.sem, Signal.START)
            pool.wait_ge(one_made, 4)
            pool.wait_ge(par_in, 16 * n_par)
            pool.wait_ge(w_bias, 2)

            chain = Chain(pool, pool_step, POOL_LINKS)

            def run(body, it):
                chain.start(body)
                for op in body.walk(it):
                    name, s, l, i = op
                    if name == "rstd":
                        pool.wait_ge(*var_ready.at(body, ("stats", s, l, 0)))
                        chain.link(nc.gpsimd.tensor_tensor(rstd[s][:, :], var[s][:, :], minus_half[:, :], ALU.pow))
                        nc.gpsimd.tensor_tensor(shift[s][:, :], shift[s][:, :], rstd[s][:, :], ALU.mult).then_inc(rstd_ready.sem, 1)
                    elif name == "affine":
                        g, b_ = (rows[f"{n}{l}"][0][:, :].unsqueeze(1).broadcast_to([P, B, D]) for n in ("g", "b_"))
                        pool.wait_ge(*xn_ready.at(body, ("apply", s, l, 0)))
                        chain.link(nc.gpsimd.tensor_tensor(xn[s][:, :, :], xn[s][:, :, :], g, ALU.mult))
                        nc.gpsimd.tensor_tensor(x[s][:, :, :], xn[s][:, :, :], b_, ALU.add).then_inc(rows_ready.sem, 1)
                    elif name == "add_row":
                        if l in ("0", "mid"):
                            pool.wait_ge(*xn_ready.at(body, ("apply", s, l, 0)))
                        elif l == 3:
                            pool.wait_ge(*filled.at(body, ("T", s, 3, 0)))
                        else:
                            pool.wait_ge(*filled.at(body, ("X", s, 4, 0)))
                        row = {"0": "bo0", "mid": "b2", 3: "bo3", 4: "bo4"}[l]
                        nc.gpsimd.tensor_tensor(x[s][:, :, :], x[s][:, :, :],
                                                rows[row][0][:, :].unsqueeze(1).broadcast_to([P, B, D]), ALU.add).then_inc(row_added.sem, 1)
                    elif name == "v_low":
                        pool.wait_ge(*v2_ready.at(body, ("v_mid", s, l, 0)))
                        nc.gpsimd.tensor_tensor(v_parts[:, 2], xn[s][:].rearrange("p b (h d) -> p (b h) d", d=HD), v_parts[:, 1], ALU.subtract).then_inc(v_ready.sem, 1)
                    elif name == "h_lo":
                        pool.wait_ge(*hi_taken.at(body, ("h_hi", s, l, i)))
                        nc.gpsimd.tensor_tensor(hT[i % 2][:, 1], h32[:, i % 2], hT[i % 2][:, 0].bitcast(F32), ALU.subtract).then_inc(h_ready.sem, 1)
                chain.end()

            run(first, 0)
            with pool.Fori(0, steps - 1) as it:
                run(loop, it)
            run(last_, 0)

        @block.tensor
        def _(pe):
            mm = nc.tensor.matmul

            def three(dst, a, b_, first, last, **kw):
                mm(dst, a(1), b_(0), start=first, stop=False, **kw)
                mm(dst, a(0), b_(1), start=False, stop=False, **kw)
                return mm(dst, a(0), b_(0), start=False, stop=last, **kw)

            pe.wait_ge(one_made, 4)
            pe.wait_ge(par_in, 16 * n_par)
            w_loads = [0] * N_STAGES
            for j, (name, src, kt, n, _) in enumerate(jobs):
                w_loads[j % N_STAGES] += 16 * (2 if isinstance(src, tuple) else 1)
                if j not in mm_rank:
                    continue
                pe.wait_ge(w_in[j % N_STAGES], w_loads[j % N_STAGES])
                if mm_rank[j] >= SLOTS:
                    pe.wait_ge(w_lo, MM_JOBS[mm_rank[j] - SLOTS] + 1)
                    pe.wait_ge(w_hi, MM_JOBS[mm_rank[j] - SLOTS] + 1)
                ps = bank[mm_rank[j] % SLOTS]
                st = staging(j)
                if name in ("q0", "k0", "v0", "w1"):
                    b_col = cols["ln2_b" if name == "w1" else "ln1_b"][0]
                    for m in range(n // P):
                        for c in range(C):
                            last = mm(ps[:, m:m + 1], st[:, c, m * P:(m + 1) * P], b_col[:, c:c + 1],
                                      start=c == 0, stop=c == C - 1)
                elif name in ("o0", "o3"):
                    pe.wait_ge(w_col, 2 if name == "o0" else 3)
                    for c in range(C):
                        last = mm(ps[:, 0:D], bv_wide[:, c, :], st[:, c, :], start=c == 0, stop=c == C - 1)
                else:
                    st2 = staging2(j)
                    for m in range(C):
                        for c in range(C):
                            last = mm(ps[:, m * D:(m + 1) * D], st[:, c, m * P:(m + 1) * P], st2[:, c, :], start=c == 0, stop=c == C - 1)
                last.then_inc(w_mm, 1)
            pe.wait_ge(w_lo, JN)

            def run(body, it):
                def took(u):
                    pe.wait_ge(*taken[bank_of[u]].at(body, taker(u)))

                def enter(u):
                    before = held_before[body, u]
                    if before is None:
                        pe.wait_ge(*taken[bank_of[u]].before(body))
                    else:
                        took(before)

                def rows_out(u, X, W):
                    for b in range(B):
                        for c in range(C):
                            last = three(flat(u)[:, b * D:(b + 1) * D], lambda p: X[:, p, c, b * P:(b + 1) * P],
                                         lambda p: W[:, p, c, :], c == 0, c == C - 1)
                    return last

                def columns_out(dst, W, m, X):
                    for c in range(C):
                        last = three(dst, lambda p: W[:, p, c, m * P:(m + 1) * P], lambda p: X[:, p, c, :], c == 0, c == C - 1)
                    return last

                for op in body.walk(it):
                    name, s, l, i = op
                    X = xT[s]
                    last = None
                    if name == "T":
                        src = x[s]
                        if l in ("0", "0m"):
                            pe.wait_ge(*xn_ready.at(body, ("apply", s, "0" if l == "0" else "mid", 0)))
                            src = xn[s]
                        elif l in ("0a", "3a"):
                            for j in range(N_ITEMS):
                                pe.wait_ge(*heads_ready.at(body, ("O_out", s, int(l[0]), j)))
                            src = xn[s]
                        elif l == 1:
                            pe.wait_ge(*taken[SLOTS].at(body, ("y_add", s, 0, 0)))
                        else:
                            pe.wait_ge(*rows_ready.at(body, ("affine", s, l - 1, 0)))
                        enter(op)
                        for c in range(C):
                            for b in range(B):
                                last = nc.tensor.transpose(halves(op)[:, c, b * P:(b + 1) * P], src[:, b, c * P:(c + 1) * P], ident[:, :])
                    elif name in ("q", "k"):
                        took(("T", s, "0" if l == 0 else l, 0))
                        enter(op)
                        for m in range(C):
                            last = columns_out(halves(op)[:, m], w[f"{name}{l}"], m, X)
                    elif name == "v":
                        took(("T", s, "0" if l == 0 else l, 0))
                        enter(op)
                        last = rows_out(op, X, w[f"v{l}"])
                    elif name == "S":
                        b, c = i // C, i % C
                        if i == 0:
                            took(("q", s, l, 0))
                            pe.wait_ge(*keys_in.at(body, ("k_move", s, l, 0)))
                        enter(op)
                        last = three(flat(op), lambda p: qT[:, p, c, b * P:(b + 1) * P],
                                     lambda p: kD[:, p, c, b].rearrange("p h k -> p (h k)"), True, True)
                    elif name == "P":
                        pe.wait_ge(*exp_ready.at(body, ("exp", s, l, i)))
                        enter(op)
                        for h in range(HC):
                            last = nc.tensor.transpose(by_head(op)[:, h], e[:, i // C, i % C, h, :], ident[:, :])
                    elif name == "O":
                        b, c = i // C, i % C
                        if i == 0:
                            pe.wait_ge(*v_ready.at(body, ("v_low", s, l, 0)))
                        took(("P", s, l, i))
                        enter(op)
                        for h in range(HC):
                            at, values = 3 * HD * h, v[:, b, c * HC + h].rearrange("p a d -> p (a d)")
                            mm(flat(op)[:, at:at + 3 * HD], p16[:, b, c, 0, h, :], values, start=True, stop=False, skip_group_check=True)
                            last = mm(flat(op)[:, at:at + 2 * HD], p16[:, b, c, 1, h, :], values[:, 0:2 * HD], start=False, stop=True,
                                      skip_group_check=True)
                    elif name == "o":
                        took(("T", s, f"{l}a", 0) if l in (0, 3) else ("X", s, l, 0))
                        enter(op)
                        last = rows_out(op, X, w[f"o{l}"])
                    elif name == "h":
                        if i == 0:
                            took(("T", s, "0m", 0))
                        enter(op)
                        for m in range(2):
                            last = columns_out(halves(op)[:, m], w["w1"], 2 * i + m, X)
                    elif name == "y":
                        pe.wait_ge(*h_ready.at(body, ("h_lo", s, l, i)))
                        if i == 0:
                            pe.wait_ge(*taken[SLOTS].at(body, ("y_add", (s - 1) % STREAMS, 0, 0)))
                        for m in range(2):
                            for b in range(B):
                                j = 2 * i + m
                                last = three(y_sum()[:, b * D:(b + 1) * D], lambda p: hT[i % 2][:, p, m, b * P:(b + 1) * P],
                                             lambda p: w["w2"][:, p, j, :], j == 0 and b == 0, j == FT - 1, skip_group_check=True)
                    elif name == "qk":
                        took(("T", s, l, 0))
                        enter(op)
                        for m in range(C):
                            if l == 4:
                                last = columns_out(halves(op)[:, m], w["q4"], m, X)
                            else:
                                last = columns_out(halves(op)[:, m], w[f"{'qk'[m]}{l}"], 0, X)
                    elif name == "S1":
                        took(("qk", s, l, 0))
                        if l == 4:
                            pe.wait_ge(*hi_taken.at(body, ("T_full", s, 4, 0)))
                        enter(op)
                        q = xn[s][:].rearrange("p b d -> p (b d)")
                        for b in range(B):
                            g = slice(b * P, (b + 1) * P)
                            pairs = [(q[:, 0:R][:, g], q[:, R:2 * R][:, g])] if l != 4 else \
                                    [(q[:, c * R:(c + 1) * R][:, g], xT_full[:, c, g]) for c in range(C)]
                            for n, (a, k) in enumerate(pairs):
                                last = mm(flat(op)[:, g], a, k, start=n == 0, stop=n == len(pairs) - 1)
                    elif name == "P1":
                        pe.wait_ge(*p_ready.at(body, ("p_norm", s, l, 0)))
                        enter(op)
                        for b in range(B):
                            last = nc.tensor.transpose(flat(op)[:, b * P:(b + 1) * P], e1[l][:, 0, b, :], ident[:, :])
                    elif name == "X":
                        took(("P1", s, l, 0))
                        enter(op)
                        for c in range(C):
                            for b in range(B):
                                last = mm(halves(op)[:, c, b * P:(b + 1) * P], x[s][:, b, c * P:(c + 1) * P], e1[l][:, 1, b, :], start=True, stop=True)
                    if last is not None:
                        last.then_inc(filled.sem, 1)

            run(first, 0)
            with pe.Fori(0, steps - 1) as it:
                run(loop, it)
            run(last_, 0)

        @block.scalar
        def _(act):
            activation = nc.scalar.activation
            pro_loads = [0] * N_STAGES
            for name, (dst, src) in rows.items():
                act.dma_start(dst[:, :], t[src].unsqueeze(0).broadcast_to([P, D])).then_inc(par_in, 16)
            act.wait_ge(par_in, 16 * n_par)
            for j, (name, src, kt, n, scale) in enumerate(jobs):
                pro_loads[j % N_STAGES] += 16 * (2 if isinstance(src, tuple) else 1)
                act.wait_ge(w_in[j % N_STAGES], pro_loads[j % N_STAGES])
                if isinstance(src, tuple):
                    act.wait_ge(w_mm, mm_rank[j] + 1)
                    last = activation(w[name][:, 0], bank[mm_rank[j] % SLOTS][:, :].rearrange("p (c d) -> p c d", c=C), ACT.Copy, scale=scale or 1.0)
                elif isinstance(scale, str):
                    if j == 0:
                        act.wait_ge(w_col, 1)
                    col = ln1_gs if scale == "ln1_gs" else cols[scale][0]
                    for c in range(kt):
                        last = activation(w[name][:, 0, c], staging(j)[:, c], ACT.Copy, scale=col[:, c:c + 1])
                else:
                    last = activation(w[name][:, 0], staging(j), ACT.Copy, scale=scale or 1.0)
                last.then_inc(w_hi, 1)
            act.wait_ge(w_lo, JN)
            act.wait_ge(w_bias, 2)


            def run(body, it):
                def read(u):
                    act.wait_ge(*filled.at(body, u))

                def taken_by(u, instruction):
                    instruction.then_inc(taken[bank_of[u]].sem, 1)

                for op in body.walk(it):
                    name, s, l, i = op
                    if name == "T_hi":
                        read(("T", s, l, 0))
                        activation(xT[s][:, 0], halves(("T", s, l, 0)), ACT.Copy).then_inc(hi_taken.sem, 1)
                    elif name == "T_full":
                        activation(xT_full, halves(("T", s, l, 0)), ACT.Copy).then_inc(hi_taken.sem, 1)
                    elif name == "X_hi":
                        read(("X", s, l, 0))
                        activation(xT[s][:, 0], halves(("X", s, l, 0)), ACT.Copy).then_inc(hi_taken.sem, 1)
                    elif name == "apply":
                        act.wait_ge(*rstd_ready.at(body, ("rstd", s, l, 0)))
                        for b in range(B):
                            last = activation(xn[s][:, b, :], x[s][:, b, :], ACT.Identity, bias=shift[s][:, b:b + 1], scale=rstd[s][:, b:b + 1])
                        last.then_inc(xn_ready.sem, 1)
                    elif name in ("q_hi", "k_hi"):
                        u = (name[0], s, l, 0)
                        dst = qT[:, 0] if name == "q_hi" else kT[:, 0].bitcast(F32R)
                        read(u)
                        for c in range(C):
                            last = activation(dst[:, c], halves(u)[:, c], ACT.Identity, bias=cols[f"b{name[0]}{l}"][0][:, c:c + 1])
                        last.then_inc(hi_taken.sem, 1)
                    elif name == "v_hi":
                        read(("v", s, l, 0))
                        activation(v_parts[:, 0], by_feature(("v", s, l, 0)), ACT.Copy).then_inc(hi_taken.sem, 1)
                    elif name == "v_mid":
                        act.wait_ge(*taken[bank_of["v", s, l, 0]].at(body, ("v_rest", s, l, 0)))
                        activation(v_parts[:, 1], xn[s][:].rearrange("p b (h d) -> p (b h) d", d=HD), ACT.Copy).then_inc(v2_ready.sem, 1)
                    elif name == "exp":
                        b, c = i // C, i % C
                        act.wait_ge(*scores_ready.at(body, ("mask", s, l, i)))
                        for h in range(HC):
                            n = c * HC + h
                            last = activation(e[:, b, c, h, :], e[:, b, c, h, :], ACT.Exp, bias=neg_max[:, b, n:n + 1], accum_out=total[:, b, n:n + 1])
                        last.then_inc(exp_ready.sem, 1)
                    elif name == "P_hi":
                        read(("P", s, l, i))
                        activation(p16[:, i // C, i % C, 0], by_head(("P", s, l, i)), ACT.Copy).then_inc(hi_taken.sem, 1)
                    elif name == "gelu":
                        u = ("h", s, l, i)
                        read(u)
                        if i >= 2:
                            act.wait_ge(*h_ready.at(body, ("h_lo", s, l, i - 2)))
                        for m in range(2):
                            last = activation(h32[:, i % 2, m], halves(u)[:, m], ACT.Gelu, bias=cols["b1"][0][:, 2 * i + m:2 * i + m + 1])
                        taken_by(u, last)
                    elif name == "h_hi":
                        act.wait_ge(*taken[bank_of["h", s, l, i]].at(body, ("gelu", s, l, i)))
                        if i >= 2:
                            read(("y", s, l, i - 2))
                        activation(hT[i % 2][:, 0], h32[:, i % 2], ACT.Copy).then_inc(hi_taken.sem, 1)
                    elif name == "qk_out":
                        u = ("qk", s, l, 0)
                        read(u)
                        dst = xn[s][:].rearrange("p b d -> p (b d)").rearrange("p (m r) -> p m r", m=2)
                        if l == 4:
                            taken_by(u, activation(dst, halves(u), ACT.Copy))
                        else:
                            activation(dst[:, 0], halves(u)[:, 0], ACT.Identity, bias=cols[f"bq{l}"][0][:, 0:1])
                            taken_by(u, activation(dst[:, 1], halves(u)[:, 1], ACT.Identity, bias=cols[f"bk{l}"][0][:, 0:1]))
                    elif name == "exp1":
                        act.wait_ge(*scores_ready.at(body, ("mask1", s, l, 0)))
                        for b in range(B):
                            last = activation(e1[l][:, 0, b, :], e1[l][:, 0, b, :], ACT.Exp, bias=neg_max1[s][:, b:b + 1],
                                              accum_out=total1[s][:, b:b + 1])
                        last.then_inc(exp_ready.sem, 1)
                    elif name == "P1_out":
                        u = ("P1", s, l, 0)
                        read(u)
                        taken_by(u, activation(e1[l][:, 1].rearrange("p b k -> p (b k)"), flat(u, R), ACT.Copy))

            run(first, 0)
            with act.Fori(0, steps - 1) as it:
                run(loop, it)
            run(last_, 0)

        @block.vector
        def _(dve):
            V = nc.vector
            pro = [0]

            def link_pro(ins):
                pro[0] += 1
                ins.then_inc(dve_pro, 1)
                dve.wait_ge(dve_pro, pro[0])

            dve.wait_ge(par_in, 16 * n_par)
            dve.wait_ge(one_made, 4)
            V.tensor_scalar(ln1_gs[:, :], cols["ln1_g"][0][:, :], scale_hd, None, ALU.mult).then_inc(w_col, 1)
            for name in ("bq1", "bq2"):
                link_pro(V.tensor_scalar(cols[name][0][:, :], cols[name][0][:, :], scale_dk, None, ALU.mult))
            link_pro(V.tensor_scalar(cols["bq3"][0][:, :], cols["bq3"][0][:, :], scale_hd, None, ALU.mult))

            def widen(col):
                for c in range(C):
                    last = V.tensor_scalar(bv_wide[:, c, :], ident[:, :], 0.0, col[:, c:c + 1], ALU.mult, ALU.add)
                last.then_inc(w_col, 1)

            for j, (name, src, kt, n, scale) in enumerate(jobs):
                if j in mm_rank:
                    dve.wait_ge(w_mm, mm_rank[j] + 1)
                    ps = bank[mm_rank[j] % SLOTS]
                    if name in ("q0", "k0", "v0", "w1"):
                        col = cols["b1" if name == "w1" else f"b{name}"][0]
                        link_pro(V.tensor_tensor(col[:, :], ps[:, 0:n // P], col[:, :], ALU.add))
                        if name == "q0":
                            link_pro(V.tensor_scalar(col[:, :], col[:, :], scale_hd, None, ALU.mult))
                    if name in ("o0", "o3"):
                        row = rows[f"b{name}"][0]
                        V.tensor_tensor(row[:, :], ps[:, 0:D], row[:, :], ALU.add).then_inc(w_bias, 1)
                dve.wait_ge(w_hi, j + 1)
                high = w[name][:, 0].bitcast(F32)
                if isinstance(src, tuple):
                    last = V.scalar_tensor_tensor(out=w[name][:, 1], in0=bank[mm_rank[j] % SLOTS][:, :].rearrange("p (c d) -> p c d", c=C), scalar=scale or 1.0,
                                                  in1=high, op0=ALU.mult, op1=ALU.subtract)
                elif isinstance(scale, str):
                    col = ln1_gs if scale == "ln1_gs" else cols[scale][0]
                    for c in range(kt):
                        last = V.scalar_tensor_tensor(out=w[name][:, 1, c], in0=staging(j)[:, c], scalar=col[:, c:c + 1],
                                                      in1=high[:, c], op0=ALU.mult, op1=ALU.subtract)
                else:
                    last = V.scalar_tensor_tensor(out=w[name][:, 1], in0=staging(j), scalar=scale or 1.0, in1=high,
                                                  op0=ALU.mult, op1=ALU.subtract)
                last.then_inc(w_lo, 1)
                if name in ("v0", "v3"):
                    if name == "v3":
                        dve.wait_ge(w_bias, 1)
                    widen(cols[f"b{name}"][0])

            chain = Chain(dve, dve_step, DVE_LINKS)
            link = chain.link

            def run(body, it):
                chain.start(body)

                def filled_by(u):
                    dve.wait_ge(*filled.at(body, u))

                def taken_by(u, instruction):
                    instruction.then_inc(taken[bank_of[u]].sem, 1)

                def low(u, dst, high, view=halves):
                    dve.wait_ge(*hi_taken.at(body, ("T_full" if u[0] == "T" and u[2] == 4 else f"{u[0]}_hi", *u[1:])))
                    taken_by(u, V.tensor_tensor(dst, view(u), high, ALU.subtract))

                def masked(u, to, view, bias_, neg):
                    filled_by(u)
                    taken_by(u, V.tensor_tensor(to, view, bias_, ALU.add))
                    took = taken[bank_of[u]]
                    dve.wait_ge(*took.at(body, taker(u)))
                    V.tensor_reduce(out=neg, in_=to, op=ALU.max, axis=AX.X, negate=True).then_inc(scores_ready.sem, 1)

                for op in body.walk(it):
                    name, s, l, i = op
                    x_flat = x[s][:].rearrange("p b d -> p (b d)")
                    if name == "bias":
                        dve.wait_ge(*adj_in[s].at(body, ("load", s, 0, 0)))
                        a, d, m = adj[s][:, :, :], bias[s][:, :, :], xn[s][:, 0].rearrange("p (b k) -> p b k", k=P)
                        V.tensor_scalar(m, a, 0.0, None, ALU.max)
                        link(V.tensor_scalar(d, a, 0.0, MASKED, ALU.is_le, ALU.mult))
                        link(V.scalar_tensor_tensor(out=m, in0=m, scalar=0.1, in1=m, op0=ALU.mult, op1=ALU.mult))
                        link(V.tensor_tensor(d, d, m, ALU.add))
                    elif name == "edges":
                        V.tensor_scalar(bias[s][:, :, :], adj[s][:, :, :], 0.0, MASKED, ALU.is_equal, ALU.mult)
                        link(V.tensor_reduce(out=has_edge[s][:, :], in_=adj[s][:, :, :], op=ALU.max, axis=AX.X, apply_absolute_value=True))
                        link(V.tensor_scalar(has_edge[s][:, :], has_edge[s][:, :], 0.0, None, ALU.not_equal))
                    elif name == "stats":
                        st, mu, gp, va = stats[s], shift[s], gap[s], var[s]
                        if l == "0":
                            dve.wait_ge(*x_in[s].at(body, ("load", s, 0, 0)))
                        for b in range(B):
                            last = V.bn_stats(st[:, b, :], x[s][:, b, :])
                        link(last)
                        even_mean, even_m2, odd_mean, odd_m2 = (st[:, :, n] for n in (1, 2, 4, 5))
                        V.tensor_tensor(mu[:, :], even_mean, odd_mean, ALU.add)
                        V.tensor_tensor(gp[:, :], even_mean, odd_mean, ALU.subtract)
                        link(V.tensor_tensor(va[:, :], even_m2, odd_m2, ALU.add))
                        V.tensor_scalar(mu[:, :], mu[:, :], -0.5, None, ALU.mult)
                        V.scalar_tensor_tensor(out=gp[:, :], in0=gp[:, :], scalar=0.25, in1=gp[:, :], op0=ALU.mult, op1=ALU.mult)
                        link(V.tensor_scalar(va[:, :], va[:, :], 1.0 / D, EPS, ALU.mult, ALU.add))
                        V.tensor_tensor(va[:, :], va[:, :], gp[:, :], ALU.add).then_inc(var_ready.sem, 1)
                    elif name == "T_lo":
                        low(("T", s, l, 0), xT[s][:, 1], xT[s][:, 0].bitcast(F32))
                    elif name == "X_lo":
                        low(("X", s, l, 0), xT[s][:, 1], xT[s][:, 0].bitcast(F32))
                    elif name in ("q_lo", "k_lo"):
                        u = (name[0], s, l, 0)
                        dst, high = (qT[:, 1], qT[:, 0].bitcast(F32)) if name == "q_lo" else (kT[:, 1].bitcast(F32R), kT[:, 0])
                        dve.wait_ge(*hi_taken.at(body, (f"{name[0]}_hi", s, l, 0)))
                        for c in range(C):
                            last = V.scalar_tensor_tensor(out=dst[:, c], in0=halves(u)[:, c], scalar=cols[f"b{name[0]}{l}"][0][:, c:c + 1],
                                                          in1=high[:, c], op0=ALU.add, op1=ALU.subtract)
                        taken_by(u, last)
                    elif name == "v_rest":
                        low(("v", s, l, 0), xn[s][:].rearrange("p b (h d) -> p (b h) d", d=HD), v_parts[:, 0], by_feature)
                    elif name == "mask":
                        b, c = i // C, i % C
                        u = ("S", s, l, i)
                        masked(u, e[:, b, c], by_head(u), bias[s][:, b, :].unsqueeze(1).broadcast_to([P, HC, P]), neg_max[:, b, c * HC:(c + 1) * HC])
                    elif name == "P_lo":
                        b, c = i // C, i % C
                        u = ("P", s, l, i)
                        dve.wait_ge(*hi_taken.at(body, ("P_hi", s, l, i)))
                        V.reciprocal(rinv[:, b, c * HC:(c + 1) * HC], total[:, b, c * HC:(c + 1) * HC])
                        low(u, p16[:, b, c, 1], p16[:, b, c, 0], by_head)
                    elif name == "O_out":
                        b, c = i // C, i % C
                        u = ("O", s, l, i)
                        filled_by(u)
                        rows_ = xn[s][:, b, c * P:(c + 1) * P].rearrange("p (h d) -> p h d", d=HD)
                        taken_by(u, V.tensor_reduce(out=rows_, in_=flat(u, 3 * P).rearrange("p (h a d) -> p h d a", a=3, d=HD), op=ALU.add, axis=AX.X))
                        dve.wait_ge(*taken[bank_of[u]].at(body, op))
                        V.tensor_tensor(rows_, rows_, rinv[:, b, c * HC:(c + 1) * HC].unsqueeze(2).broadcast_to([P, HC, HD]),
                                        ALU.mult).then_inc(heads_ready.sem, 1)
                    elif name == "o_add":
                        u = ("o", s, l, 0)
                        if l in (0, 3, 4):
                            dve.wait_ge(*row_added.at(body, ("add_row", s, "0" if l == 0 else l, 0)))
                        filled_by(u)
                        taken_by(u, V.tensor_tensor(x_flat, flat(u), x_flat, ALU.add))
                        dve.wait_ge(*taken[bank_of[u]].at(body, op))
                    elif name == "y_add":
                        dve.wait_ge(*row_added.at(body, ("add_row", s, "mid", 0)))
                        filled_by(("y", s, 0, N_TILES - 1))
                        V.tensor_tensor(x_flat, y_sum(), x_flat, ALU.add).then_inc(taken[SLOTS].sem, 1)
                    elif name == "mask1":
                        u = ("S1", s, l, 0)
                        masked(u, e1[l][:, 0], flat(u, R).rearrange("p (b k) -> p b k", b=B), bias[s][:, :, :], neg_max1[s][:, :])
                    elif name == "p_norm":
                        dve.wait_ge(*exp_ready.at(body, ("exp1", s, l, 0)))
                        link(V.reciprocal(rinv1[s][:, :], total1[s][:, :]))
                        edge = one_each if l == 4 else has_edge[s]
                        link(V.tensor_tensor(rinv1[s][:, :], rinv1[s][:, :], edge[:, :], ALU.mult))
                        p = e1[l][:, 0]
                        V.tensor_tensor(p, p, rinv1[s][:, :].unsqueeze(2).broadcast_to([P, B, P]), ALU.mult).then_inc(p_ready.sem, 1)
                chain.end()

            run(first, 0)
            with dve.Fori(0, steps - 1) as it:
                run(loop, it)
            run(last_, 0)


LAYERED = {"L1_gnn_Wq": True, "L1_gnn_Wk": True, "L1_gnn_Wc": True, "L1_gnn_bq": False, "L1_gnn_bk": False,
           "L1_gnn_ln_g": False, "L1_gnn_ln_b": False}
COLUMNS = ("L0_gnn_ln1_g", "L0_gnn_ln1_b", "L0_gnn_ln2_g", "L0_gnn_ln2_b", "L0_gnn_bq", "L0_gnn_bk", "L0_gnn_bv", "L0_gnn_b1",
           "L1_gnn_bq0", "L1_gnn_bk0", "L1_gnn_bq1", "L1_gnn_bk1", "L2_gnn_bq", "L2_gnn_bk", "L2_gnn_bv")
TRANSPOSED = ("L3_gnn_Wq", "L3_gnn_Wk", "L3_gnn_Wv")


def laid_out(inputs):
    arrays = {}
    for name, a in inputs.items():
        a = np.asarray(a)
        if name in LAYERED:
            for n in range(a.shape[0]):
                arrays[f"{name}{'T' if LAYERED[name] else ''}{n}"] = np.ascontiguousarray(a[n].T)
        elif name in TRANSPOSED:
            arrays[f"{name}T"] = np.ascontiguousarray(a.T)
        else:
            arrays[name] = np.ascontiguousarray(a)
    for name in COLUMNS:
        arrays[name + "_col"] = np.ascontiguousarray(arrays.pop(name).reshape(-1, P).T)
    return arrays


def kernel(**inputs):
    import concourse.bacc as bacc
    from concourse.bass_utils import run_bass_kernel_spmd

    nc = bacc.Bacc("TRN2", target_bir_lowering=False, num_devices=1)
    arrays = laid_out(inputs)
    t = {n: nc.dram_tensor(f"in_{n}", a.shape, mybir.dt.from_np(a.dtype), kind="ExternalInput").ap() for n, a in arrays.items()}
    graphs = arrays["x"].shape[0]
    out = nc.dram_tensor("out", (graphs, P, D), F32, kind="ExternalOutput").ap()
    mk_kernel(nc, graphs // (B * STREAMS), t, out)
    r = run_bass_kernel_spmd(nc, [{f"in_{n}": a for n, a in arrays.items()}], core_ids=[0])
    return r.results[0]["out"]
```
